# Optimizing a Trainium2 kernel written in Bass

```python
import numpy as np
import jax
import jax.numpy as jnp

def _softmax(x, axis=-1):
    return jax.nn.softmax(x, axis=axis)

def _gelu(x):
    return jax.nn.gelu(x, approximate=True)

def _silu(x):
    return jax.nn.silu(x)

def _sigmoid(x):
    return jax.nn.sigmoid(x)

def _layernorm(x, axis=-1, eps=1e-05):
    m = jnp.mean(x, axis=axis, keepdims=True)
    v = jnp.var(x, axis=axis, keepdims=True)
    return (x - m) / jnp.sqrt(v + eps)

def _scatter_add(tgt, idx, src, axis=0):
    return tgt.at[idx].add(src)

def _segment_sum(src, seg, n):
    return jax.ops.segment_sum(src, seg, n)
kernel_name = 'mk_adj_resnorm_d2_adj_r2_a84031'

def setup_inputs(seed: int=0):
    np.random.seed(seed)
    _w = jnp.asarray

    def _rec_inputs():
        import jax
        import jax.numpy as jnp
        _gk = jax.random.key(seed)
        x = -0.0003929 + 0.9999 * jax.random.normal(jax.random.fold_in(_gk, 1), (16, 512, 256), jnp.float32)
        _a = jax.random.bernoulli(jax.random.fold_in(_gk, 2), 0.015625, (16, 512, 512))
        _a = jnp.logical_or(_a, jnp.swapaxes(_a, -1, -2))
        _a = jnp.logical_or(_a, jnp.eye(512, dtype=bool))
        _af = _a.astype(jnp.float32)
        _af = _af * jax.random.uniform(jax.random.fold_in(_gk, 3), (16, 512, 512), jnp.float32, 0.05, 1)
        adj = _af
        return (x, adj)
    x, adj = _rec_inputs()

    def _L0_gnn_setup():
        import jax, jax.numpy as jnp
        import numpy as np
        B, N, F_IN, F_HID, F_OUT = (32, 512, 256, 256, 256)

        def _gcn_layer(x, adj, W, b):
            support = jnp.einsum('bnf,fh->bnh', x, W)
            return jnp.einsum('bnm,bmh->bnh', adj, support) + b
        key = jax.random.key(seed)
        ks = jax.random.split(key, 8)

        def xavier(k, fan_in, fan_out):
            bound = float(np.sqrt(6.0 / (fan_in + fan_out)))
            return jax.random.uniform(k, (fan_in, fan_out), jnp.float32, -bound, bound)
        return {'batch_graph': jax.random.normal(ks[0], (B, N, F_IN), jnp.float32), 'adj': jax.random.uniform(ks[1], (B, N, N), jnp.float32), 'W1': xavier(ks[2], F_IN, F_HID), 'b1': jnp.zeros((F_HID,), jnp.float32), 'W2': xavier(ks[3], F_HID, F_HID), 'b2': jnp.zeros((F_HID,), jnp.float32), 'W3': xavier(ks[4], F_HID, F_OUT), 'b3': jnp.zeros((F_OUT,), jnp.float32)}
    _L0_gnn_all = _L0_gnn_setup()
    _L0_gnn_in = {k: v for k, v in _L0_gnn_all.items() if k in ('W1', 'b1', 'W2', 'b2', 'W3', 'b3')}
    del _L0_gnn_all

    def _L1_gnn_setup():
        import jax, jax.numpy as jnp
        import numpy as np
        EMBED_DIM = 256
        NUM_HEADS = 8
        HEAD_DIM = EMBED_DIM // NUM_HEADS
        SCALE = HEAD_DIM ** (-0.5)
        B, S = (16, 512)
        key = jax.random.key(seed)
        ks = jax.random.split(key, 12)
        init = lambda k, shape: jax.random.normal(k, shape, dtype=jnp.float32) * EMBED_DIM ** (-0.5)
        return {'x': jax.random.normal(ks[0], (B, S, EMBED_DIM), dtype=jnp.float32), 'adj_matrix': jax.random.uniform(ks[1], (B, S, S), dtype=jnp.float32), 'bond_matrix': jax.random.uniform(ks[2], (B, S, S), dtype=jnp.float32), 'Wq': init(ks[3], (EMBED_DIM, EMBED_DIM)), 'bq': jnp.zeros((EMBED_DIM,), jnp.float32), 'Wk': init(ks[4], (EMBED_DIM, EMBED_DIM)), 'bk': jnp.zeros((EMBED_DIM,), jnp.float32), 'Wv': init(ks[5], (EMBED_DIM, EMBED_DIM)), 'bv': jnp.zeros((EMBED_DIM,), jnp.float32), 'Wo': init(ks[6], (EMBED_DIM, EMBED_DIM)), 'bo': jnp.zeros((EMBED_DIM,), jnp.float32), 'seq_len': S}
    _L1_gnn_all = _L1_gnn_setup()
    _L1_gnn_in = {k: v for k, v in _L1_gnn_all.items() if k in ('Wq', 'bq', 'Wk', 'bk', 'Wv', 'bv', 'Wo', 'bo')}
    del _L1_gnn_all
    return {'x': x, 'adj': adj, 'L0_gnn_W1': _L0_gnn_in['W1'], 'L0_gnn_b1': _L0_gnn_in['b1'], 'L0_gnn_W2': _L0_gnn_in['W2'], 'L0_gnn_b2': _L0_gnn_in['b2'], 'L0_gnn_W3': _L0_gnn_in['W3'], 'L0_gnn_b3': _L0_gnn_in['b3'], 'L1_gnn_Wq': _L1_gnn_in['Wq'], 'L1_gnn_bq': _L1_gnn_in['bq'], 'L1_gnn_Wk': _L1_gnn_in['Wk'], 'L1_gnn_bk': _L1_gnn_in['bk'], 'L1_gnn_Wv': _L1_gnn_in['Wv'], 'L1_gnn_bv': _L1_gnn_in['bv'], 'L1_gnn_Wo': _L1_gnn_in['Wo'], 'L1_gnn_bo': _L1_gnn_in['bo']}

def reference(x, adj, L0_gnn_W1, L0_gnn_b1, L0_gnn_W2, L0_gnn_b2, L0_gnn_W3, L0_gnn_b3, L1_gnn_Wq, L1_gnn_bq, L1_gnn_Wk, L1_gnn_bk, L1_gnn_Wv, L1_gnn_bv, L1_gnn_Wo, L1_gnn_bo):
    import jax
    import jax.numpy as jnp

    def _L0_gnn_ref(batch_graph, adj, W1, b1, W2, b2, W3, b3):
        import jax, jax.numpy as jnp
        import numpy as np
        B, N, F_IN, F_HID, F_OUT = (32, 512, 256, 256, 256)

        def _gcn_layer(x, adj, W, b):
            support = jnp.einsum('bnf,fh->bnh', x, W)
            return jnp.einsum('bnm,bmh->bnh', adj, support) + b
        x = jax.nn.relu(_gcn_layer(batch_graph, adj, W1, b1))
        x = jax.nn.relu(_gcn_layer(x, adj, W2, b2))
        out = _gcn_layer(x, adj, W3, b3)
        return out

    def _L1_gnn_ref(x, adj_matrix, bond_matrix, Wq, bq, Wk, bk, Wv, bv, Wo, bo, seq_len):
        import jax, jax.numpy as jnp
        import numpy as np
        EMBED_DIM = 256
        NUM_HEADS = 8
        HEAD_DIM = EMBED_DIM // NUM_HEADS
        SCALE = HEAD_DIM ** (-0.5)
        B, S = (16, 512)
        b = x.shape[0]

        def proj(W, bias):
            y = jnp.einsum('bse,fe->bsf', x, W) + bias
            return y.reshape(b, seq_len, NUM_HEADS, HEAD_DIM).transpose(0, 2, 1, 3)
        q, k, v = (proj(Wq, bq), proj(Wk, bk), proj(Wv, bv))
        scores = jnp.einsum('bhqd,bhkd->bhqk', q, k) * SCALE
        mask = (adj_matrix + bond_matrix)[:, None, :, :]
        scores = scores * mask
        attn = jax.nn.softmax(scores, axis=-1)
        ctx = jnp.einsum('bhqk,bhkd->bhqd', attn, v)
        ctx = ctx.transpose(0, 2, 1, 3).reshape(b, seq_len, EMBED_DIM)
        return jnp.einsum('bse,fe->bsf', ctx, Wo) + bo
    x = _layernorm(x + _L0_gnn_ref(x, adj, L0_gnn_W1, L0_gnn_b1, L0_gnn_W2, L0_gnn_b2, L0_gnn_W3, L0_gnn_b3), axis=-1)
    x = _layernorm(x + _L1_gnn_ref(x, adj, adj, L1_gnn_Wq, L1_gnn_bq, L1_gnn_Wk, L1_gnn_bk, L1_gnn_Wv, L1_gnn_bv, L1_gnn_Wo, L1_gnn_bo, 512), axis=-1)
    return x

_drawn_inputs = setup_inputs


def setup_inputs(seed=0):
    import zlib

    import numpy as np

    out = dict(_drawn_inputs(seed))
    spreads = {'L0_gnn_b1': (0.0, 0.1),
     'L0_gnn_b2': (0.0, 0.8),
     'L0_gnn_b3': (0.0, 2.0),
     'L1_gnn_bq': (0.0, 2.0),
     'L1_gnn_bk': (0.0, 2.0),
     'L1_gnn_bv': (0.0, 0.1),
     'L1_gnn_bo': (0.0, 0.1)}
    factors = {'L1_gnn_Wq': 8.0, 'L1_gnn_Wk': 8.0}
    for name, (base, spread) in spreads.items():
        noise = np.random.default_rng([zlib.crc32(name.encode()), seed]).standard_normal(out[name].shape)
        drawn = base * np.exp(spread * noise) if base else spread * noise
        out[name] = jnp.asarray(drawn.astype(out[name].dtype))
    for name, factor in factors.items():
        out[name] = (out[name] * factor).astype(out[name].dtype)
    return out
```

```python
from contextlib import ExitStack

import numpy as np

import concourse.bass as bass
from concourse import mybir

F32 = mybir.dt.float32
F32R = mybir.dt.float32r
ALU = mybir.AluOpType
ACT = mybir.ActivationFunctionType

P = 128
HEADS = 8
EPS = 1e-5

ADJ_T, AX, H1, S2, H2, S3, OUT3, X_T, K0, Q0, V, K1, Q1 = 0, 4, 6, 8, 10, 12, 14, 16, 18, 19, 20, 22, 23
JOBS = 24
JOB_BANKS = 3
JOB_SLOT = [0, 0, 1, 1, 3, 4, 6, 7, 9, 10, 12, 13, 15, 16, 18, 19, 22, 22, 24, 25, 26, 27, 28, 29]
RELU_JOBS = (H1, H1 + 1, H2, H2 + 1)
VECTOR_ONLY = (OUT3, OUT3 + 1, V, V + 1)
SCALAR_JOBS = [j for j in range(JOBS) if j not in VECTOR_ONLY]

TRANSPOSE_LAG = 2
RINV_LAG, PV_LAG, CTX_LAG, WO_LAG, Y2_LAG, NORM2_LAG = 5, 6, 6, 7, 7, 8
DRAIN_SLOTS = 6


def gcn_attention_kernel(nc, x, adj, W1, b1, W2, b2, W3, b3, Wq, bq, Wk, bk, Wv, bv, Wo, bo, out):
    B, N, F = x.shape
    NT, FC = N // P, F // P
    DH = F // HEADS
    GROUP = P // DH
    GROUPS = HEADS // GROUP
    SLOTS = HEADS * NT
    STEPS = SLOTS // GROUP
    TERMS = P // DH
    assert (NT, FC, DH, GROUP, GROUPS, TERMS) == (4, 2, 32, 4, 2, 4)
    SCORE_SCALE = 2.0 * DH ** -0.5
    STACK_DMAS = 2 * TERMS * GROUP
    ACT_COPIES = 3

    x_v = x.rearrange("b (t p) f -> b p t f", p=P)
    adj_v = adj.rearrange("b (t p) m -> b p t m", p=P)
    out_v = out.rearrange("b (t p) f -> b p t f", p=P)

    with ExitStack() as ctx:
        def sb(name, shape, dt=F32):
            return ctx.enter_context(nc.sbuf_tensor(name, shape, dt))

        def sem(name):
            return ctx.enter_context(nc.semaphore(name))

        ident = sb("ident", [P, P])
        adj_in = sb("adj_in", [P, NT, N])
        mask = sb("mask", [P, NT, N])
        adjT = [sb(f"adjT_{k}", [P, NT, N], F32R) for k in "hl"]
        x_in = sb("x_in", [P, NT, F])
        xs = [sb(f"xs_{k}", [P, NT * F], F32R) for k in "hl"]
        xb = sb("xb", [P, NT, F])
        prod = [sb(f"prod_{k}", [P, NT * F], F32R) for k in "hl"]
        hid = sb("hid", [P, FC, N])
        hids = [sb(f"hids_{k}", [P, FC, N], F32R) for k in "hl"]
        y1 = sb("y1", [P, 2, 2, F])
        xn = sb("xn", [P, NT, F])
        res = sb("res", [P, NT, F])
        qk = {t: [sb(f"{t}_{k}", [P, GROUPS, N], F32R) for k in "hl"] for t in "qk"}
        stack = {t: sb(f"{t}_stack", [P, HEADS, N], F32R) for t in "qk"}
        v_new = sb("v_new", [P, NT, F])
        v_use = sb("v_use", [P, NT, F])
        masked = sb("masked", [P, 2, N])
        probs = sb("probs", [P, 4, N])
        probsT = sb("probsT", [P, 2, GROUP, N])
        ctxT = sb("ctxT", [P, GROUPS, NT, P])
        rinvT = sb("rinvT", [P, P])
        y2 = sb("y2", [P, 2, F])
        out_sb = sb("out_sb", [P, 2, F])
        w_gcn = [sb(f"w_gcn_{k}", [P, 3, FC, F], F32R) for k in "hl"]
        w_qkv = [sb(f"w_qkv_{k}", [P, 3, FC, F], F32R) for k in "hl"]
        w_o = sb("w_o", [P, FC, F])
        b_cols = sb("b_cols", [P, 4, FC])
        b_rows = sb("b_rows", [P, 3, F])
        rowmax = sb("rowmax", [P, GROUP])
        shift = sb("shift", [P, GROUP])
        rowsum = sb("rowsum", [P, 2, GROUP])
        rinv = sb("rinv", [P, 2, GROUP])
        rinv_wide = sb("rinv_wide", [P, P])
        stats1 = sb("stats1", [P, 2, 2, 6])
        mv1 = sb("mv1", [P, 2, 2, 2])
        ve1 = sb("ve1", [P, 2, 2])
        rstd1 = sb("rstd1", [P, 2, 2])
        stats2 = sb("stats2", [P, 2, 6])
        mv2 = sb("mv2", [P, 2, 2])
        ve2 = sb("ve2", [P, 2, 1])
        rstd2 = sb("rstd2", [P, 2, 1])
        minus_half = sb("minus_half", [P, 2])
        staged = probsT[:, :, :, :].rearrange("p a h n -> p (a h n)")[:, 0:7 * FC * F]\
            .rearrange("p (w c f) -> p w c f", w=7, c=FC)

        b_staged = masked[0:4 * FC, 0, 0:P]

        def ps(name):
            return ctx.enter_context(nc.psum_tensor(name, [P, N], F32))

        score_ps = [ps("score0"), ps("score1")]
        turn_ps = [ps("turn0"), ps("turn1")]
        ctx_ps = ps("ctx_ps")
        ctx_acc, rinv_ps, wo_ps = ctx_ps[:, 0:P], ctx_ps[:, P:2 * P], ctx_ps[:, 2 * P:2 * P + F]
        job_ps = [ps(f"job{k}") for k in range(JOB_BANKS)]

        w_loaded = sem("w_loaded")
        ident_zero, ident_ready = sem("ident_zero"), sem("ident_ready")
        w_turned, w_hi, w_ready = sem("w_turned"), sem("w_hi"), sem("w_ready")
        x_loaded, adj_loaded = sem("x_loaded"), sem("adj_loaded")
        mask_loaded = [sem(f"mask_loaded{t}") for t in range(NT)]
        stack_ready = [sem(f"stack_ready{g}") for g in range(GROUPS)]
        v_ready = [sem(f"v_ready{g}") for g in range(GROUPS)]
        out_stored = [sem(f"out_stored{k}") for k in range(2)]
        x_hi, x_lo, xb_ready, res_ready = sem("x_hi"), sem("x_lo"), sem("xb_ready"), sem("res_ready")
        job_made, job_hi, job_done = sem("job_made"), sem("job_hi"), sem("job_done")
        hid_hi = sem("hid_hi")
        y1_ready, stats1_ready, mv1_ready = sem("y1_ready"), sem("stats1_ready"), sem("mv1_ready")
        ve1_ready, rstd1_ready, xn_ready = sem("ve1_ready"), sem("rstd1_ready"), sem("xn_ready")
        scores_made, masked_ready, shift_ready = sem("scores_made"), sem("masked_ready"), sem("shift_ready")
        probs_ready, turned = sem("probs_ready"), sem("turned")
        copied_act, copied_dve = sem("copied_act"), sem("copied_dve")
        rinv_raw, rinv_ready, pv_made, rinvT_ready, ctx_ready = (
            sem("rinv_raw"), sem("rinv_ready"), sem("pv_made"), sem("rinvT_ready"), sem("ctx_ready"))
        wo_made, y2_ready, stats2_ready, mv2_ready = (
            sem("wo_made"), sem("y2_ready"), sem("stats2_ready"), sem("mv2_ready"))
        ve2_ready, rstd2_ready, out_ready = sem("ve2_ready"), sem("rstd2_ready"), sem("out_ready")

        def exists(graph):
            b, off = graph
            return not isinstance(b, int) or 0 <= b + off < B

        def due(graph, per_graph, count):
            b, off = graph
            n = b * per_graph + (off * per_graph + count)
            return None if isinstance(n, int) and n <= 0 else n

        def held(eng, value):
            return eng.to_reg(value) if value is not None and not isinstance(value, int) else value

        def ago(b, slot, lag):
            return ((b, 0), slot - lag) if slot >= lag else ((b, -1), slot - lag + SLOTS)

        def iterations(eng, iteration, last_looped):
            iteration(-1)
            iteration(0)
            with eng.Fori(1, last_looped + 1) as b:
                iteration(b)
            for b in range(last_looped + 1, B):
                iteration(b)
            iteration(B)

        def slots(b):
            return range(DRAIN_SLOTS + 4 if isinstance(b, int) and b == B else SLOTS)

        def jobs_in(slot):
            return [j for j in range(JOBS) if JOB_SLOT[j] == slot]

        def scalar_count(j):
            return sum(k <= j for k in SCALAR_JOBS)

        def act_copies(slot):
            return ACT_COPIES * (slot // GROUP) + min(slot % GROUP, ACT_COPIES)

        def split_target(j):
            if j < AX:
                return [t[:, j, :] for t in adjT]
            if j < H1:
                return [t[:, (j - AX) * N:(j - AX + 1) * N] for t in prod]
            if S2 <= j < H2:
                return [t[:, (j - S2) * N:(j - S2 + 1) * N] for t in prod]
            if S3 <= j < OUT3:
                return [t[:, (j - S3) * N:(j - S3 + 1) * N] for t in prod]
            if X_T <= j < K0:
                return [t[:, (j - X_T) * N:(j - X_T + 1) * N] for t in xs]
            raise ValueError(j)

        block = ctx.enter_context(nc.Block())

        @block.sync
        def _(sp):
            for n, w in enumerate((W1, W2, W3, Wq, Wk, Wv, Wo)):
                sp.dma_start(staged[:, n, :, :], w.rearrange("(c p) f -> p c f", p=P)).then_inc(w_loaded, 16)
            sp.dma_start(x_in[:], x_v[0]).then_inc(x_loaded, 16)
            sp.dma_start(adj_in[:], adj_v[0]).then_inc(adj_loaded, 16)
            for n, v in enumerate((b1, b2, bq, bk)):
                sp.dma_start(b_staged[FC * n:FC * (n + 1), :], v.rearrange("(c p) -> c p", p=P)).then_inc(w_loaded, 16)
            for n, v in enumerate((b3, bv, bo)):
                sp.dma_start(b_rows[:, n, :], v.partition_broadcast(P)).then_inc(w_loaded, 16)

            def load_inputs(b):
                graph = (b, 2)
                if not exists(graph):
                    return
                n = held(sp, due((b, 1), JOBS, ADJ_T + NT))
                sp.wait_ge(ident_ready, 1)
                sp.wait_ge(job_made, n)
                sp.dma_start(adj_in[:], adj_v[b + 2]).then_inc(adj_loaded, 16)
                n = held(sp, due((b, 1), NT, NT))
                sp.wait_ge(ident_ready, 1)
                sp.wait_ge(xb_ready, n)
                sp.dma_start(x_in[:], x_v[b + 2]).then_inc(x_loaded, 16)

            def load_mask(b, t):
                if exists((b, 1)):
                    if (n := held(sp, due((b, 0), SLOTS, SLOTS - (NT - 1 - t) * GROUP))) is not None:
                        sp.wait_ge(ident_ready, 1)
                        sp.wait_ge(masked_ready, n)
                    sp.dma_start(mask[:, t, :], adj_v[b + 1, :, t, :]).then_inc(mask_loaded[t], 16)

            def stack_group(b, g):
                if exists((b, 1)):
                    n = held(sp, due((b, 1), JOBS, (Q0, Q1)[g] + 1))
                    sp.wait_ge(ident_ready, 1)
                    sp.wait_ge(job_done, n)
                    if (n := held(sp, due((b, 0), SLOTS, SLOTS // GROUPS * (g + 1)))) is not None:
                        sp.wait_ge(ident_ready, 1)
                        sp.wait_ge(scores_made, n)
                    for term in range(TERMS):
                        for t in "qk":
                            part = qk[t][term % 2 if t == "q" else term // 2]
                            for h in range(GROUP):
                                sp.dma_start(
                                    stack[t][DH * term:DH * (term + 1), GROUP * g + h, :].bitcast(F32),
                                    part[DH * h:DH * (h + 1), g, :].bitcast(F32)).then_inc(stack_ready[g], 16)

            def copy_v(b, g):
                if exists((b, 1)):
                    n = held(sp, due((b, 1), JOBS, V + 2))
                    sp.wait_ge(ident_ready, 1)
                    sp.wait_ge(job_done, n)
                    if (n := held(sp, due((b, 0), STEPS, NT * (g + 1)))) is not None:
                        sp.wait_ge(ident_ready, 1)
                        sp.wait_ge(pv_made, n)
                    cols = slice(g * P, (g + 1) * P)
                    sp.dma_start(v_use[:, :, cols], v_new[:, :, cols]).then_inc(v_ready[g], 16)

            def store(graph, t):
                if exists(graph):
                    b, off = graph
                    n = held(sp, due(graph, NT, t + 1))
                    sp.wait_ge(ident_ready, 1)
                    sp.wait_ge(out_ready, n)
                    sp.dma_start(out_v[b + off, :, t, :], out_sb[:, t % 2, :]).then_inc(out_stored[t % 2], 16)

            def iteration(b):
                load_mask_of_previous = not isinstance(b, int) or b >= 0
                if load_mask_of_previous:
                    stack_group(b - 1, 1)
                    load_mask(b - 1, NT - 1)
                    store((b, -1), 2)
                load_first = not isinstance(b, int) or b >= -1
                if load_first:
                    load_inputs(b)
                if load_mask_of_previous:
                    copy_v(b - 1, 1)
                    store((b, -1), 3)
                if isinstance(b, int) and b == B:
                    return
                load_mask(b, 0)
                store((b, 0), 0)
                load_mask(b, 1)
                stack_group(b, 0)
                copy_v(b, 0)
                store((b, 0), 1)
                load_mask(b, 2)

            iterations(sp, iteration, B - 3)
            for k in range(2):
                n = held(sp, due((B - 1, 0), 16 * NT // 2, 16 * NT // 2))
                sp.wait_ge(ident_ready, 1)
                sp.wait_ge(out_stored[k], n)

        @block.tensor
        def _(pe):
            def three(dst, lhs, rhs, chunks):
                terms = [(i, j, c) for c in range(chunks) for i, j in ((0, 0), (0, 1), (1, 0))]
                for n, (i, j, c) in enumerate(terms):
                    last = pe.matmul(dst, lhs(i, c), rhs(j, c), start=(n == 0), stop=(n == len(terms) - 1))
                return last

            x_part = [t[:].rearrange("p (t f) -> p t f", t=NT) for t in xs]
            xT_part = [t[:].rearrange("p (c n) -> p c n", c=FC) for t in xs]
            axT_part = [t[:].rearrange("p (c n) -> p c n", c=FC) for t in prod]
            sup_part = [t[:].rearrange("p (t f) -> p t f", t=NT) for t in prod]

            pe.wait_ge(w_loaded, 16 * 14)
            pe.wait_ge(ident_ready, 1)
            for n, bank in enumerate((*job_ps, score_ps[0])):
                for e in range(FC):
                    for c in range(FC):
                        last = pe.transpose(bank[:, (FC * e + c) * P:(FC * e + c + 1) * P],
                                            staged[:, 3 + n, c, e * P:(e + 1) * P], ident[:])
                last.then_inc(w_turned, 1)
            pe.transpose(score_ps[1][:, 0:4 * FC], b_staged, ident[0:4 * FC, 0:4 * FC]).then_inc(w_turned, 1)

            def job(b, j):
                graph = (b, 1)
                if not exists(graph):
                    return
                bank = job_ps[j % JOB_BANKS]
                if (n := due(graph, JOBS, j - JOB_BANKS + 1)) is not None:
                    pe.wait_ge(job_done, n)
                if j == ADJ_T:
                    pe.wait_ge(adj_loaded, due(graph, 16, 16))
                needs = {AX: ADJ_T + NT, H1: H1, S2: S2, H2: H2, S3: S3, OUT3: OUT3, K0: X_T + FC}.get(j)
                if needs is not None:
                    pe.wait_ge(job_done, due(graph, JOBS, needs))
                if j < AX:
                    for t in range(NT):
                        last = pe.transpose(bank[:, t * P:(t + 1) * P],
                                            adj_in[:, t, j * P:(j + 1) * P], ident[:])
                elif j < H1:
                    if j == AX:
                        pe.wait_ge(x_hi, due(graph, 1, 1))
                        pe.wait_ge(x_lo, due(graph, NT, NT))
                    f = j - AX
                    last = three(bank[:], lambda i, m: x_part[i][:, m, f * P:(f + 1) * P],
                                 lambda i, m: adjT[i][:, m, :], NT)
                elif j < S2:
                    f = j - H1
                    last = three(bank[:], lambda i, c: w_gcn[i][:, 0, c, f * P:(f + 1) * P],
                                 lambda i, c: axT_part[i][:, c, :], FC)
                elif j < H2 or S3 <= j < OUT3:
                    layer = 1 if j < H2 else 2
                    for t in range(2):
                        n = 2 * (j - (S2 if j < H2 else S3)) + t
                        last = three(bank[:, t * F:(t + 1) * F],
                                     lambda i, c: hids[i][:, c, n * P:(n + 1) * P],
                                     lambda i, c: w_gcn[i][:, layer, c, :], FC)
                elif j < S3:
                    f = j - H2
                    last = three(bank[:], lambda i, m: sup_part[i][:, m, f * P:(f + 1) * P],
                                 lambda i, m: adjT[i][:, m, :], NT)
                elif j < X_T:
                    for t in range(2):
                        n = 2 * (j - OUT3) + t
                        last = three(bank[:, t * F:(t + 1) * F],
                                     lambda i, m: adjT[i][:, m, n * P:(n + 1) * P],
                                     lambda i, m: sup_part[i][:, m, :], NT)
                elif j < K0:
                    if j == X_T:
                        pe.wait_ge(xn_ready, due(graph, NT, NT))
                    for t in range(NT):
                        last = pe.transpose(bank[:, t * P:(t + 1) * P],
                                            xn[:, t, (j - X_T) * P:(j - X_T + 1) * P], ident[:])
                elif j in (V, V + 1):
                    for t in range(2):
                        n = 2 * (j - V) + t
                        last = three(bank[:, t * F:(t + 1) * F],
                                     lambda i, c: xT_part[i][:, c, n * P:(n + 1) * P],
                                     lambda i, c: w_qkv[i][:, 2, c, :], FC)
                else:
                    g = 0 if j < V else 1
                    w = 0 if j in (Q0, Q1) else 1
                    last = three(bank[:], lambda i, c: w_qkv[i][:, w, c, g * P:(g + 1) * P],
                                 lambda i, c: xT_part[i][:, c, :], FC)
                last.then_inc(job_made, 1)

            def scores(b, i):
                graph = (b, 0)
                if not exists(graph):
                    return
                step, h = divmod(i, GROUP)
                g, t = divmod(step, NT)
                if i % (SLOTS // GROUPS) == 0:
                    pe.wait_ge(stack_ready[g], due(graph, 16 * STACK_DMAS, 16 * STACK_DMAS))
                if (n := due(graph, SLOTS, i - 1)) is not None:
                    pe.wait_ge(masked_ready, n)
                head = GROUP * g + h
                pe.matmul(score_ps[i % 2][:], stack["q"][:, head, t * P:(t + 1) * P],
                          stack["k"][:, head, :], start=True, stop=True).then_inc(scores_made, 1)

            def turn(b, i):
                graph, k = ago(b, i, TRANSPOSE_LAG)
                if not exists(graph):
                    return
                pe.wait_ge(probs_ready, due(graph, SLOTS, k + 1))
                if (k - 2) % GROUP < ACT_COPIES:
                    if (n := due(graph, ACT_COPIES * STEPS, act_copies(k - 1))) is not None:
                        pe.wait_ge(copied_act, n)
                else:
                    if (n := due(graph, STEPS, (k - 1) // GROUP)) is not None:
                        pe.wait_ge(copied_dve, n)
                for c in range(NT):
                    last = pe.transpose(turn_ps[k % 2][:, c * P:(c + 1) * P],
                                        probs[:, k % 4, c * P:(c + 1) * P], ident[:])
                last.then_inc(turned, 1)

            def context(b, i):
                if (i - PV_LAG) % GROUP:
                    return
                graph, k = ago(b, i, PV_LAG)
                if not exists(graph):
                    return
                step = k // GROUP
                g, t = divmod(step, NT)
                pe.wait_ge(copied_act, due(graph, ACT_COPIES * STEPS, ACT_COPIES * (step + 1)))
                pe.wait_ge(copied_dve, due(graph, STEPS, step + 1))
                if t == 0:
                    pe.wait_ge(v_ready[g], due(graph, 16, 16))
                if (n := due(graph, STEPS, step)) is not None:
                    pe.wait_ge(ctx_ready, n)
                if (n := due(graph, NT, max(step - NT, 0))) is not None:
                    pe.wait_ge(y2_ready, n)
                for c in range(NT):
                    for h in range(GROUP):
                        col = g * P + DH * h
                        pe.matmul(ctx_acc[DH * h:DH * (h + 1), :], v_use[:, c, col:col + DH],
                                  probsT[:, step % 2, h, c * P:(c + 1) * P],
                                  start=(c == 0), stop=(c == NT - 1), tile_position=(0, DH * h))
                pe.wait_ge(rinv_ready, due(graph, STEPS, step + 1))
                pe.transpose(rinv_ps, rinv_wide[:], ident[:]).then_inc(pv_made, 1)

            def out_product(b, i):
                if (i - WO_LAG) % GROUP:
                    return
                graph, k = ago(b, i, WO_LAG)
                step = k // GROUP
                g, t = divmod(step, NT)
                if not exists(graph) or g != GROUPS - 1:
                    return
                pe.wait_ge(ctx_ready, due(graph, STEPS, step + 1))
                for e in range(FC):
                    last = pe.matmul(wo_ps, ctxT[:, e, t, :], w_o[:, e, :], start=(e == 0), stop=(e == FC - 1))
                last.then_inc(wo_made, 1)

            def iteration(b):
                for i in slots(b):
                    scores(b, i)
                    turn(b, i)
                    context(b, i)
                    out_product(b, i)
                    for j in jobs_in(i):
                        job(b, j)

            pe.wait_ge(w_ready, 6)
            iterations(pe, iteration, B - 2)

        @block.scalar
        def _(act):
            def copy_turned(b, i):
                graph, k = ago(b, i, TRANSPOSE_LAG)
                step, h = divmod(k, GROUP)
                if not exists(graph) or h >= ACT_COPIES:
                    return
                act.wait_ge(turned, due(graph, SLOTS, k + 1))
                if (n := due(graph, STEPS, step - 1)) is not None:
                    act.wait_ge(pv_made, n)
                act.activation(probsT[:, step % 2, h, :], turn_ps[k % 2][:], ACT.Copy).then_inc(copied_act, 1)

            def exponentials(b, i):
                graph = (b, 0)
                if not exists(graph):
                    return
                step, h = divmod(i, GROUP)
                act.wait_ge(shift_ready, due(graph, SLOTS, i + 1))
                if (n := due(graph, SLOTS, i - 3)) is not None:
                    act.wait_ge(turned, n)
                if h == 0:
                    if (n := due(graph, STEPS, step - 1)) is not None:
                        act.wait_ge(rinv_raw, n)
                act.activation(probs[:, i % 4, :], masked[:, i % 2, :], ACT.Exp, bias=shift[:, h:h + 1],
                               scale=SCORE_SCALE, accum_out=rowsum[:, step % 2, h:h + 1]).then_inc(probs_ready, 1)

            def job(b, j):
                graph = (b, 1)
                if not exists(graph) or j in VECTOR_ONLY:
                    return
                bank = job_ps[j % JOB_BANKS][:]
                act.wait_ge(job_made, due(graph, JOBS, j + 1))
                if j in RELU_JOBS:
                    layer, f = (0, j - H1) if j < S2 else (1, j - H2)
                    if (n := due(graph, JOBS, S2 if layer else H2 + 2 - JOBS)) is not None:
                        act.wait_ge(job_done, n)
                    act.activation(hid[:, f, :], bank, ACT.Relu, bias=b_cols[:, layer, f:f + 1]).then_inc(job_hi, 1)
                elif j in (K0, Q0, K1, Q1):
                    g = 0 if j < V else 1
                    t = "q" if j in (Q0, Q1) else "k"
                    if (n := due(graph, 16 * STACK_DMAS, 0)) is not None:
                        act.wait_ge(stack_ready[g], n)
                    act.activation(qk[t][0][:, g, :], bank, ACT.Identity,
                                   bias=b_cols[:, 2 + (t == "k"), g:g + 1]).then_inc(job_hi, 1)
                else:
                    act.activation(split_target(j)[0], bank, ACT.Copy).then_inc(job_hi, 1)

            def iteration(b):
                for i in slots(b):
                    copy_turned(b, i)
                    exponentials(b, i)
                    for j in jobs_in(i):
                        job(b, j)

            act.wait_ge(w_ready, 6)
            iterations(act, iteration, B - 2)

        @block.vector
        def _(dve):
            dve.wait_ge(w_loaded, 16 * 14)
            dve.tensor_copy(w_gcn[0][:], staged[:, 0:3, :, :]).then_inc(w_hi, 1)
            dve.wait_ge(w_hi, 1)
            dve.tensor_tensor(w_gcn[1][:], staged[:, 0:3, :, :], w_gcn[0][:].bitcast(F32),
                              ALU.subtract).then_inc(w_ready, 1)
            for n, bank in enumerate((*job_ps, score_ps[0])):
                turned_w = bank[:].rearrange("p (e f) -> p e f", e=FC)
                dve.wait_ge(w_turned, n + 1)
                if n < 3:
                    dve.tensor_copy(w_qkv[0][:, n, :, :], turned_w).then_inc(w_hi, 1)
                    dve.wait_ge(w_hi, n + 2)
                    dve.tensor_tensor(w_qkv[1][:, n, :, :], turned_w, w_qkv[0][:, n, :, :].bitcast(F32),
                                      ALU.subtract).then_inc(w_ready, 1)
                else:
                    dve.tensor_copy(w_o[:], turned_w).then_inc(w_ready, 1)

            dve.wait_ge(w_turned, 5)
            dve.tensor_copy(b_cols[:].rearrange("p n c -> p (n c)"), score_ps[1][:, 0:4 * FC]).then_inc(w_ready, 1)

            def mask_scores(b, i):
                graph = (b, 0)
                if not exists(graph):
                    return
                t = i // GROUP % NT
                made = held(dve, due(graph, SLOTS, i + 1))
                used = held(dve, due(graph, SLOTS, i - 1))
                loaded = held(dve, due(graph, 16, 16))
                dve.wait_ge(ident_ready, 1)
                dve.wait_ge(scores_made, made)
                if used is not None:
                    dve.wait_ge(probs_ready, used)
                if i % GROUP == 0 and i < SLOTS // GROUPS:
                    dve.wait_ge(mask_loaded[t], loaded)
                dve.tensor_tensor_reduce(masked[:, i % 2, :], score_ps[i % 2][:], mask[:, t, :], 1.0,
                                         float(np.finfo(np.float32).min), ALU.mult, ALU.max,
                                         rowmax[:, i % GROUP:i % GROUP + 1]).then_inc(masked_ready, 1)

            def copy_turned(b, i):
                graph, k = ago(b, i, TRANSPOSE_LAG)
                step, h = divmod(k, GROUP)
                if not exists(graph) or h < ACT_COPIES:
                    return
                dve.wait_ge(turned, due(graph, SLOTS, k + 1))
                if (n := due(graph, STEPS, step - 1)) is not None:
                    dve.wait_ge(pv_made, n)
                dve.tensor_copy(probsT[:, step % 2, h, :], turn_ps[k % 2][:]).then_inc(copied_dve, 1)

            def reciprocals(b, i):
                if (i - RINV_LAG) % GROUP:
                    return
                graph, k = ago(b, i, RINV_LAG)
                if not exists(graph):
                    return
                step = k // GROUP
                dve.wait_ge(probs_ready, due(graph, SLOTS, GROUP * (step + 1)))
                dve.reciprocal(rinv[:, step % 2, :], rowsum[:, step % 2, :]).then_inc(rinv_raw, 1)
                dve.wait_ge(rinv_raw, due(graph, STEPS, step + 1))
                if (n := due(graph, STEPS, step)) is not None:
                    dve.wait_ge(pv_made, n)
                dve.tensor_copy(rinv_wide[:].rearrange("p (h d) -> p h d", h=GROUP),
                                rinv[:, step % 2, :].unsqueeze(2).to_broadcast([P, GROUP, DH]))\
                    .then_inc(rinv_ready, 1)

            def normalise_context(b, i):
                if (i - CTX_LAG) % GROUP:
                    return
                graph, k = ago(b, i, CTX_LAG)
                if not exists(graph):
                    return
                step = k // GROUP
                g, t = divmod(step, NT)
                dve.wait_ge(pv_made, due(graph, STEPS, step + 1))
                dve.tensor_copy(rinvT[:], rinv_ps).then_inc(rinvT_ready, 1)
                dve.wait_ge(rinvT_ready, due(graph, STEPS, step + 1))
                dve.tensor_tensor(ctxT[:, g, t, :], ctx_acc, rinvT[:], ALU.mult).then_inc(ctx_ready, 1)

            def residual2(b, i):
                if (i - Y2_LAG) % GROUP:
                    return
                graph, k = ago(b, i, Y2_LAG)
                g, t = divmod(k // GROUP, NT)
                if not exists(graph) or g != GROUPS - 1:
                    return
                dve.wait_ge(wo_made, due(graph, NT, t + 1))
                dve.wait_ge(res_ready, due(graph, NT, NT))
                dve.tensor_tensor(y2[:, t % 2, :], wo_ps, res[:, t, :], ALU.add).then_inc(y2_ready, 1)
                dve.wait_ge(y2_ready, due(graph, NT, t + 1))
                dve.bn_stats(stats2[:, t % 2, :], y2[:, t % 2, :]).then_inc(stats2_ready, 1)
                n = held(dve, due(graph, NT, t + 1))
                dve.wait_ge(ident_ready, 1)
                dve.wait_ge(stats2_ready, n)
                dve.bn_aggr(mv2[:, t % 2, :], stats2[:, t % 2, :]).then_inc(mv2_ready, 1)

            def normalise2(b, i):
                if (i - NORM2_LAG) % GROUP:
                    return
                graph, k = ago(b, i, NORM2_LAG)
                g, t = divmod(k // GROUP, NT)
                if not exists(graph) or g != GROUPS - 1:
                    return
                dve.wait_ge(rstd2_ready, due(graph, NT, t + 1))
                if (n := due(graph, 16 * NT // 2, 16 * (t // 2))) is not None:
                    dve.wait_ge(out_stored[t % 2], n)
                dve.tensor_scalar(out_sb[:, t % 2, :], y2[:, t % 2, :], mv2[:, t % 2, 0:1], rstd2[:, t % 2, 0:1],
                                  ALU.subtract, ALU.mult).then_inc(out_ready, 1)

            def split_x(b):
                graph = (b, 1)
                if exists(graph):
                    dve.wait_ge(x_loaded, due(graph, 16, 16))
                    if (n := due(graph, JOBS, 0)) is not None:
                        dve.wait_ge(job_made, n)
                    dve.tensor_copy(xs[0][:], x_in[:].rearrange("p t f -> p (t f)")).then_inc(x_hi, 1)

            def job(b, j):
                graph = (b, 1)
                if not exists(graph):
                    return
                bank = job_ps[j % JOB_BANKS][:]
                if j in VECTOR_ONLY:
                    dve.wait_ge(job_made, due(graph, JOBS, j + 1))
                else:
                    dve.wait_ge(job_hi, due(graph, len(SCALAR_JOBS), scalar_count(j)))
                if j in RELU_JOBS:
                    f = j - (H1 if j < S2 else H2)
                    order = (H1, H1 + 1, H2, H2 + 1).index(j)
                    dve.tensor_copy(hids[0][:, f, :], hid[:, f, :]).then_inc(hid_hi, 1)
                    dve.wait_ge(hid_hi, due(graph, len(RELU_JOBS), order + 1))
                    dve.tensor_tensor(hids[1][:, f, :], hid[:, f, :], hids[0][:, f, :].bitcast(F32),
                                      ALU.subtract).then_inc(job_done, 1)
                elif j in (K0, Q0, K1, Q1):
                    g = 0 if j < V else 1
                    t = "q" if j in (Q0, Q1) else "k"
                    dve.scalar_tensor_tensor(out=qk[t][1][:, g, :], in0=bank,
                                             scalar=b_cols[:, 2 + (t == "k"), g:g + 1],
                                             in1=qk[t][0][:, g, :].bitcast(F32),
                                             op0=ALU.add, op1=ALU.subtract).then_inc(job_done, 1)
                elif j in (V, V + 1):
                    for g in range(GROUPS):
                        if (n := due(graph, 16, 0)) is not None:
                            dve.wait_ge(v_ready[g], n)
                    n = 2 * (j - V)
                    dve.tensor_tensor(v_new[:, n:n + 2, :], bank.rearrange("p (t f) -> p t f", t=2),
                                      b_rows[:, 1:2, :].to_broadcast([P, 2, F]), ALU.add).then_inc(job_done, 1)
                elif j in (OUT3, OUT3 + 1):
                    a = j - OUT3
                    dve.wait_ge(xb_ready, due(graph, NT, 2 * a + 2))
                    dve.tensor_tensor(y1[:, a, :, :], bank.rearrange("p (t f) -> p t f", t=2),
                                      xb[:, 2 * a:2 * a + 2, :], ALU.add).then_inc(job_done, 1)
                    dve.wait_ge(job_done, due(graph, JOBS, j + 1))
                    for t in range(2):
                        dve.bn_stats(stats1[:, a, t, :], y1[:, a, t, :]).then_inc(stats1_ready, 1)
                    for t in range(2):
                        n = held(dve, due(graph, NT, 2 * a + t + 1))
                        dve.wait_ge(ident_ready, 1)
                        dve.wait_ge(stats1_ready, n)
                        dve.bn_aggr(mv1[:, a, t, :], stats1[:, a, t, :]).then_inc(mv1_ready, 1)
                else:
                    hi, lo = split_target(j)
                    dve.tensor_tensor(lo, bank, hi.bitcast(F32), ALU.subtract).then_inc(job_done, 1)

            def normalise1(b, a):
                graph = (b, 1)
                if not exists(graph):
                    return
                dve.wait_ge(rstd1_ready, due(graph, 2, a + 1))
                if (n := due(graph, NT, 0)) is not None:
                    dve.wait_ge(res_ready, n)
                for t in range(2):
                    dve.tensor_scalar(xn[:, 2 * a + t, :], y1[:, a, t, :], mv1[:, a, t, 0:1],
                                      rstd1[:, a, t:t + 1], ALU.subtract, ALU.mult).then_inc(xn_ready, 1)

            def iteration(b):
                for i in slots(b):
                    mask_scores(b, i)
                    if i == 0:
                        split_x(b)
                    copy_turned(b, i)
                    reciprocals(b, i)
                    normalise_context(b, i)
                    residual2(b, i)
                    normalise2(b, i)
                    for a in range(2):
                        if JOB_SLOT[OUT3 + a] + 1 == i:
                            normalise1(b, a)
                    for j in jobs_in(i):
                        job(b, j)

            iterations(dve, iteration, B - 2)

        @block.gpsimd
        def _(pool):
            pool.memset(ident[:], 0.0).then_inc(ident_zero, 1)
            pool.memset(minus_half[:], -0.5).then_inc(ident_zero, 1)
            pool.wait_ge(ident_zero, 2)
            pool.affine_select(out=ident[:], in_=ident[:], compare_op=ALU.not_equal, fill=1.0, base=0,
                               pattern=[[-1, P]], channel_multiplier=1).then_inc(ident_ready, 1)

            def shifts(b, i):
                graph = (b, 0)
                if exists(graph):
                    h = i % GROUP
                    n = held(pool, due(graph, SLOTS, i + 1))
                    pool.wait_ge(ident_ready, 1)
                    pool.wait_ge(masked_ready, n)
                    pool.tensor_scalar(shift[:, h:h + 1], rowmax[:, h:h + 1], -SCORE_SCALE, None,
                                       ALU.mult).then_inc(shift_ready, 1)

            def lo_of_x(b, t):
                graph = (b, 1)
                if exists(graph):
                    pool.wait_ge(x_hi, due(graph, 1, 1))
                    cols = slice(t * F, (t + 1) * F)
                    pool.tensor_tensor(xs[1][:, cols], x_in[:, t, :], xs[0][:, cols].bitcast(F32),
                                       ALU.subtract).then_inc(x_lo, 1)

            def x_with_bias(b, t):
                graph = (b, 1)
                if exists(graph):
                    if (n := due(graph, JOBS, OUT3 + 2 - JOBS)) is not None:
                        pool.wait_ge(job_done, n)
                    pool.tensor_tensor(xb[:, t, :], x_in[:, t, :], b_rows[:, 0, :], ALU.add).then_inc(xb_ready, 1)

            def residual(b, t):
                graph = (b, 0)
                if exists(graph):
                    pool.wait_ge(xn_ready, due(graph, NT, NT))
                    if (n := due(graph, NT, 0)) is not None:
                        pool.wait_ge(y2_ready, n)
                    pool.tensor_tensor(res[:, t, :], xn[:, t, :], b_rows[:, 2, :], ALU.add).then_inc(res_ready, 1)

            def rstd_1(b, a):
                graph = (b, 1)
                if exists(graph):
                    n = held(pool, due(graph, NT, 2 * a + 2))
                    pool.wait_ge(ident_ready, 1)
                    pool.wait_ge(mv1_ready, n)
                    pool.tensor_scalar(ve1[:, a, :], mv1[:, a, :, 1], EPS, None, ALU.add).then_inc(ve1_ready, 1)
                    pool.wait_ge(ve1_ready, due(graph, 2, a + 1))
                    pool.tensor_tensor(rstd1[:, a, :], ve1[:, a, :], minus_half[:], ALU.pow).then_inc(rstd1_ready, 1)

            def rstd_2(b, i):
                if (i - Y2_LAG) % GROUP:
                    return
                graph, k = ago(b, i, Y2_LAG)
                g, t = divmod(k // GROUP, NT)
                if not exists(graph) or g != GROUPS - 1:
                    return
                n = held(pool, due(graph, NT, t + 1))
                pool.wait_ge(ident_ready, 1)
                pool.wait_ge(mv2_ready, n)
                pool.tensor_scalar(ve2[:, t % 2, :], mv2[:, t % 2, 1:2], EPS, None, ALU.add).then_inc(ve2_ready, 1)
                pool.wait_ge(ve2_ready, due(graph, NT, t + 1))
                pool.tensor_tensor(rstd2[:, t % 2, :], ve2[:, t % 2, :], minus_half[:, 0:1],
                                   ALU.pow).then_inc(rstd2_ready, 1)

            def iteration(b):
                for i in slots(b):
                    shifts(b, i)
                    rstd_2(b, i)
                    if i < 2:
                        lo_of_x(b, 2 * i)
                        lo_of_x(b, 2 * i + 1)
                    elif 4 <= i < 8:
                        x_with_bias(b, i - 4)
                    elif 9 <= i < 13:
                        residual(b, i - 9)
                    for a in range(2):
                        if JOB_SLOT[OUT3 + a] == i:
                            rstd_1(b, a)

            pool.wait_ge(w_loaded, 16 * 14)
            iterations(pool, iteration, B - 2)


_INS = ["x", "adj", "L0_gnn_W1", "L0_gnn_b1", "L0_gnn_W2", "L0_gnn_b2", "L0_gnn_W3", "L0_gnn_b3",
        "L1_gnn_Wq", "L1_gnn_bq", "L1_gnn_Wk", "L1_gnn_bk", "L1_gnn_Wv", "L1_gnn_bv", "L1_gnn_Wo", "L1_gnn_bo"]


def kernel(**inputs):
    import concourse.bacc as _bacc
    from concourse.bass_utils import run_bass_kernel_spmd as _run

    nc = _bacc.Bacc("TRN2", target_bir_lowering=False, num_devices=1)
    arrays, args = {}, []
    for name in _INS:
        a = np.ascontiguousarray(inputs[name])
        arrays[f"in_{name}"] = a
        args.append(nc.dram_tensor(f"in_{name}", a.shape, mybir.dt.from_np(a.dtype), kind="ExternalInput").ap())
    out = nc.dram_tensor("out", inputs["x"].shape, F32, kind="ExternalOutput").ap()
    gcn_attention_kernel(nc, *args, out)
    r = _run(nc, [arrays], core_ids=[0])
    return r.results[0]["out"]
```

```python
from contextlib import ExitStack

import numpy as np

import concourse.bass as bass
from concourse import mybir

F32 = mybir.dt.float32
F32R = mybir.dt.float32r
ALU = mybir.AluOpType
ACT = mybir.ActivationFunctionType

P = 128
HEADS = 8
EPS = 1e-5

ADJ_T, AX, H1, S2, H2, S3, OUT3, X_T, K0, Q0, V, K1, Q1 = 0, 4, 6, 8, 10, 12, 14, 16, 18, 19, 20, 22, 23
JOBS = 24
JOB_BANKS = 3
PARTS = [2 if j in (AX, AX + 1, H2, H2 + 1, OUT3, OUT3 + 1) else 1 for j in range(JOBS)]
PLAN = {
    0: [(0, 0), (1, 0)], 1: [(2, 0), (3, 0)],
    2: [(AX, 0)], 3: [(AX, 1)], 4: [(AX + 1, 0)], 6: [(AX + 1, 1)],
    7: [(H1, 0)], 8: [(H1 + 1, 0)],
    10: [(S2, 0)], 11: [(S2 + 1, 0)],
    12: [(H2, 0)], 14: [(H2, 1)], 15: [(H2 + 1, 0)], 16: [(H2 + 1, 1)],
    18: [(S3, 0)], 19: [(S3 + 1, 0)],
    20: [(OUT3, 0)], 21: [(OUT3, 1)], 22: [(OUT3 + 1, 0)], 23: [(OUT3 + 1, 1)],
    26: [(X_T, 0), (X_T + 1, 0)],
    27: [(K0, 0)], 28: [(Q0, 0)], 29: [(V, 0)], 30: [(V + 1, 0), (K1, 0)], 31: [(Q1, 0)],
}
assert [x for i in sorted(PLAN) for x in PLAN[i]] == [(j, k) for j in range(JOBS) for k in range(PARTS[j])]
RELU_JOBS = (H1, H1 + 1, H2, H2 + 1)
VECTOR_ONLY = (OUT3, OUT3 + 1, V, V + 1)
SCALAR_JOBS = [j for j in range(JOBS) if j not in VECTOR_ONLY]

EXP_LAG, TRANSPOSE_LAG = 1, 4
RINV_LAG, PV_LAG, CTX_LAG, WO_LAG, Y2_LAG, STATS2_LAG, NORM2_LAG = 6, 9, 9, 10, 10, 11, 12
STATS1_LAG, NORM1_LAG = 1, 2
DRAIN_SLOTS = NORM2_LAG - 3


def gcn_attention_kernel(nc, x, adj, W1, b1, W2, b2, W3, b3, Wq, bq, Wk, bk, Wv, bv, Wo, bo, out):
    B, N, F = x.shape
    NT, FC = N // P, F // P
    DH = F // HEADS
    GROUP = P // DH
    GROUPS = HEADS // GROUP
    SLOTS = HEADS * NT
    STEPS = SLOTS // GROUP
    TERMS = P // DH
    assert (NT, FC, DH, GROUP, GROUPS, TERMS) == (4, 2, 32, 4, 2, 4)
    SCORE_SCALE = 2.0 * DH ** -0.5
    STACK_DMAS = 2 * TERMS
    ACT_COPIES = 3

    x_v = x.rearrange("b (t p) f -> b p t f", p=P)
    adj_v = adj.rearrange("b (t p) m -> b p t m", p=P)
    out_v = out.rearrange("b (t p) f -> b p t f", p=P)

    with ExitStack() as ctx:
        def sb(name, shape, dt=F32):
            return ctx.enter_context(nc.sbuf_tensor(name, shape, dt))

        def sem(name):
            return ctx.enter_context(nc.semaphore(name))

        ident = sb("ident", [P, P])
        adj_in = sb("adj_in", [P, NT, N])
        mask = sb("mask", [P, NT, N])
        adjT = [sb(f"adjT_{k}", [P, NT, N], F32R) for k in "hl"]
        x_in = sb("x_in", [P, NT, F])
        xs = [sb(f"xs_{k}", [P, NT * F], F32R) for k in "hl"]
        xb = sb("xb", [P, NT, F])
        prod = [sb(f"prod_{k}", [P, NT * F], F32R) for k in "hl"]
        hid = sb("hid", [P, FC, N])
        hids = [sb(f"hids_{k}", [P, FC, N], F32R) for k in "hl"]
        y1 = sb("y1", [P, 2, 2, F])
        xn = sb("xn", [P, NT, F])
        res = sb("res", [P, NT, F])
        qk = {t: [sb(f"{t}_{k}", [P, GROUPS, N], F32R) for k in "hl"] for t in "qk"}
        stack = {t: sb(f"{t}_stack", [P, HEADS, N], F32R) for t in "qk"}
        v_new = sb("v_new", [P, NT, F])
        v_use = sb("v_use", [P, NT, F])
        masked = sb("masked", [P, 2, N])
        probs = sb("probs", [P, 4, N])
        probsT = sb("probsT", [P, 2, GROUP, N])
        ctxT = sb("ctxT", [P, GROUPS, NT, P])
        rinvT = sb("rinvT", [P, P])
        y2 = sb("y2", [P, 2, F])
        out_sb = sb("out_sb", [P, 2, F])
        w_gcn = [sb(f"w_gcn_{k}", [P, 3, FC, F], F32R) for k in "hl"]
        w_qkv = [sb(f"w_qkv_{k}", [P, 3, FC, F], F32R) for k in "hl"]
        w_o = sb("w_o", [P, FC, F])
        b_cols = sb("b_cols", [P, 4, FC])
        b_rows = sb("b_rows", [P, 3, F])
        rowmax = sb("rowmax", [P, GROUP])
        shift = sb("shift", [P, GROUP])
        rowsum = sb("rowsum", [P, 2, GROUP])
        rinv = sb("rinv", [P, 2, GROUP])
        rinv_wide = sb("rinv_wide", [P, P])
        stats1 = sb("stats1", [P, 2, 2, 6])
        mv1 = sb("mv1", [P, 2, 2, 2])
        ve1 = sb("ve1", [P, 2, 2])
        rstd1 = sb("rstd1", [P, 2, 2])
        stats2 = sb("stats2", [P, 2, 6])
        mv2 = sb("mv2", [P, 2, 2])
        ve2 = sb("ve2", [P, 2, 1])
        rstd2 = sb("rstd2", [P, 2, 1])
        minus_half = sb("minus_half", [P, 2])
        staged = probsT[:, :, :, :].rearrange("p a h n -> p (a h n)")[:, 0:7 * FC * F]\
            .rearrange("p (w c f) -> p w c f", w=7, c=FC)

        b_staged = masked[0:2 * FC, :, 0:P]
        b_by_feature = masked[0:2 * FC, 0, P:2 * P]

        def ps(name):
            return ctx.enter_context(nc.psum_tensor(name, [P, N], F32))

        score_ps = [ps("score0"), ps("score1")]
        turn_ps = [ps("turn0"), ps("turn1")]
        ctx_ps = ps("ctx_ps")
        ctx_acc, rinv_ps, wo_ps = ctx_ps[:, 0:P], ctx_ps[:, P:2 * P], ctx_ps[:, 2 * P:2 * P + F]
        job_ps = [ps(f"job{k}") for k in range(JOB_BANKS)]

        w_loaded = sem("w_loaded")
        ident_zero, ident_ready = sem("ident_zero"), sem("ident_ready")
        b_ordered = sem("b_ordered")
        w_turned, w_hi, w_ready = sem("w_turned"), sem("w_hi"), sem("w_ready")
        x_loaded, adj_loaded = sem("x_loaded"), sem("adj_loaded")
        mask_loaded = [sem(f"mask_loaded{t}") for t in range(NT)]
        stack_ready = [sem(f"stack_ready{g}") for g in range(GROUPS)]
        v_ready = [sem(f"v_ready{g}") for g in range(GROUPS)]
        out_stored = [sem(f"out_stored{k}") for k in range(2)]
        x_hi, x_lo, xb_ready, res_ready = sem("x_hi"), sem("x_lo"), sem("xb_ready"), sem("res_ready")
        job_made, job_hi, job_done = sem("job_made"), sem("job_hi"), sem("job_done")
        hid_hi = sem("hid_hi")
        stats1_ready, mv1_ready = sem("stats1_ready"), sem("mv1_ready")
        ve1_ready, rstd1_ready, xn_ready = sem("ve1_ready"), sem("rstd1_ready"), sem("xn_ready")
        scores_made, masked_ready, shift_ready = sem("scores_made"), sem("masked_ready"), sem("shift_ready")
        probs_ready, turned = sem("probs_ready"), sem("turned")
        copied_act, copied_dve = sem("copied_act"), sem("copied_dve")
        rinv_raw, rinv_ready, pv_made, rinvT_ready, ctx_ready = (
            sem("rinv_raw"), sem("rinv_ready"), sem("pv_made"), sem("rinvT_ready"), sem("ctx_ready"))
        wo_made, y2_ready, stats2_ready, mv2_ready = (
            sem("wo_made"), sem("y2_ready"), sem("stats2_ready"), sem("mv2_ready"))
        ve2_ready, rstd2_ready, out_ready = sem("ve2_ready"), sem("rstd2_ready"), sem("out_ready")

        def exists(graph):
            b, off = graph
            return not isinstance(b, int) or 0 <= b + off < B

        def due(graph, per_graph, count):
            b, off = graph
            n = b * per_graph + (off * per_graph + count)
            return None if isinstance(n, int) and n <= 0 else n

        def held(eng, value):
            return eng.to_reg(value) if value is not None and not isinstance(value, int) else value

        def ago(b, slot, lag):
            return ((b, 0), slot - lag) if slot >= lag else ((b, -1), slot - lag + SLOTS)

        def iterations(eng, iteration, last_looped):
            iteration(-1)
            iteration(0)
            with eng.Fori(1, last_looped + 1) as b:
                iteration(b)
            for b in range(last_looped + 1, B):
                iteration(b)
            iteration(B)

        def slots(b):
            return range(DRAIN_SLOTS if isinstance(b, int) and b == B else SLOTS)

        def jobs_in(slot):
            return [j for j, part in PLAN.get(slot, []) if part == PARTS[j] - 1]

        def scalar_count(j):
            return sum(k <= j for k in SCALAR_JOBS)

        def act_copies(slot):
            return ACT_COPIES * (slot // GROUP) + min(slot % GROUP, ACT_COPIES)

        def split_target(j):
            if j < AX:
                return [t[:, j, :] for t in adjT]
            if j < H1:
                return [t[:, (j - AX) * N:(j - AX + 1) * N] for t in prod]
            if S2 <= j < H2:
                return [t[:, (j - S2) * N:(j - S2 + 1) * N] for t in prod]
            if S3 <= j < OUT3:
                return [t[:, (j - S3) * N:(j - S3 + 1) * N] for t in prod]
            if X_T <= j < K0:
                return [t[:, (j - X_T) * N:(j - X_T + 1) * N] for t in xs]
            raise ValueError(j)

        block = ctx.enter_context(nc.Block())

        @block.sync
        def _(sp):
            for n, w in enumerate((W1, W2, W3, Wq, Wk, Wv, Wo)):
                sp.dma_start(staged[:, n, :, :], w.rearrange("(c p) f -> p c f", p=P)).then_inc(w_loaded, 16)
            sp.dma_start(x_in[:], x_v[0]).then_inc(x_loaded, 16)
            sp.dma_start(adj_in[:], adj_v[0]).then_inc(adj_loaded, 16)
            for n, v in enumerate((b1, b2, bq, bk)):
                sp.dma_start(b_staged[FC * (n % 2):FC * (n % 2 + 1), n // 2, :], v.rearrange("(c p) -> c p", p=P)).then_inc(w_loaded, 16)
            for n, v in enumerate((b3, bv, bo)):
                sp.dma_start(b_rows[:, n, :], v.partition_broadcast(P)).then_inc(w_loaded, 16)

            def load_inputs(b):
                graph = (b, 2)
                if not exists(graph):
                    return
                n = held(sp, due((b, 1), JOBS, ADJ_T + NT))
                sp.wait_ge(ident_ready, 1)
                sp.wait_ge(job_made, n)
                sp.dma_start(adj_in[:], adj_v[b + 2]).then_inc(adj_loaded, 16)
                n = held(sp, due((b, 1), NT, NT))
                sp.wait_ge(ident_ready, 1)
                sp.wait_ge(xb_ready, n)
                sp.dma_start(x_in[:], x_v[b + 2]).then_inc(x_loaded, 16)

            def load_mask(b, t):
                if exists((b, 1)):
                    if (n := held(sp, due((b, 0), SLOTS, SLOTS - (NT - 1 - t) * GROUP))) is not None:
                        sp.wait_ge(ident_ready, 1)
                        sp.wait_ge(masked_ready, n)
                    sp.dma_start(mask[:, t, :], adj_v[b + 1, :, t, :]).then_inc(mask_loaded[t], 16)

            def stack_group(b, g):
                if exists((b, 1)):
                    n = held(sp, due((b, 1), JOBS, (Q0, Q1)[g] + 1))
                    sp.wait_ge(ident_ready, 1)
                    sp.wait_ge(job_done, n)
                    if (n := held(sp, due((b, 0), SLOTS, SLOTS // GROUPS * (g + 1)))) is not None:
                        sp.wait_ge(ident_ready, 1)
                        sp.wait_ge(scores_made, n)
                    for term in range(TERMS):
                        for t in "qk":
                            part = qk[t][term % 2 if t == "q" else term // 2]
                            sp.dma_start(
                                stack[t][DH * term:DH * (term + 1), GROUP * g:GROUP * (g + 1), :].bitcast(F32),
                                part[:, g, :].bitcast(F32)).then_inc(stack_ready[g], 16)

            def copy_v(b, g):
                if exists((b, 1)):
                    n = held(sp, due((b, 1), JOBS, V + 2))
                    sp.wait_ge(ident_ready, 1)
                    sp.wait_ge(job_done, n)
                    if (n := held(sp, due((b, 0), STEPS, NT * (g + 1)))) is not None:
                        sp.wait_ge(ident_ready, 1)
                        sp.wait_ge(pv_made, n)
                    cols = slice(g * P, (g + 1) * P)
                    sp.dma_start(v_use[:, :, cols], v_new[:, :, cols]).then_inc(v_ready[g], 16)

            def store(graph, t):
                if exists(graph):
                    b, off = graph
                    n = held(sp, due(graph, NT, t + 1))
                    sp.wait_ge(ident_ready, 1)
                    sp.wait_ge(out_ready, n)
                    sp.dma_start(out_v[b + off, :, t, :], out_sb[:, t % 2, :]).then_inc(out_stored[t % 2], 16)

            def iteration(b):
                load_mask_of_previous = not isinstance(b, int) or b >= 0
                if load_mask_of_previous:
                    stack_group(b - 1, 1)
                    load_mask(b - 1, NT - 1)
                    store((b, -1), 2)
                load_first = not isinstance(b, int) or b >= -1
                if load_first:
                    load_inputs(b)
                if load_mask_of_previous:
                    copy_v(b - 1, 1)
                    store((b, -1), 3)
                if isinstance(b, int) and b == B:
                    return
                load_mask(b, 0)
                store((b, 0), 0)
                load_mask(b, 1)
                stack_group(b, 0)
                copy_v(b, 0)
                store((b, 0), 1)
                load_mask(b, 2)

            iterations(sp, iteration, B - 3)
            for k in range(2):
                n = held(sp, due((B - 1, 0), 16 * NT // 2, 16 * NT // 2))
                sp.wait_ge(ident_ready, 1)
                sp.wait_ge(out_stored[k], n)

        @block.tensor
        def _(pe):
            def three(dst, lhs, rhs, chunks, part=0, parts=1, sources=None):
                for c in range(chunks // parts * part, chunks // parts * (part + 1)):
                    if sources is not None:
                        graph, of_chunk = sources
                        pe.wait_ge(job_done, due(graph, JOBS, of_chunk[c] + 1))
                    for i, j in ((0, 0), (0, 1), (1, 0)):
                        last = pe.matmul(dst, lhs(i, c), rhs(j, c), start=(c == 0 and i + j == 0),
                                         stop=(c == chunks - 1 and i == 1))
                return last

            x_part = [t[:].rearrange("p (t f) -> p t f", t=NT) for t in xs]
            xT_part = [t[:].rearrange("p (c n) -> p c n", c=FC) for t in xs]
            axT_part = [t[:].rearrange("p (c n) -> p c n", c=FC) for t in prod]
            sup_part = [t[:].rearrange("p (t f) -> p t f", t=NT) for t in prod]

            pe.wait_ge(w_loaded, 16 * 14)
            pe.wait_ge(ident_ready, 1)
            for n, bank in enumerate((*job_ps, score_ps[0])):
                for e in range(FC):
                    for c in range(FC):
                        last = pe.transpose(bank[:, (FC * e + c) * P:(FC * e + c + 1) * P],
                                            staged[:, 3 + n, c, e * P:(e + 1) * P], ident[:])
                last.then_inc(w_turned, 1)
            pe.transpose(score_ps[1][:, 0:2 * FC], b_staged[:, 0, :], ident[0:2 * FC, 0:2 * FC])
            pe.wait_ge(b_ordered, 1)
            pe.transpose(score_ps[1][:, 2 * FC:4 * FC], b_by_feature,
                         ident[0:2 * FC, 0:2 * FC]).then_inc(w_turned, 1)

            def job(b, j, part):
                graph = (b, 1)
                if not exists(graph):
                    return
                bank = job_ps[j % JOB_BANKS]
                if part == 0 and (n := due(graph, JOBS, j - JOB_BANKS + 1)) is not None:
                    pe.wait_ge(job_done, n)
                if j == ADJ_T:
                    pe.wait_ge(adj_loaded, due(graph, 16, 16))
                by_chunk = {AX: (0, 1, 2, 3), H1: (AX, AX + 1), S2: (H1, H1 + 1), H2: (S2, S2, S2 + 1, S2 + 1),
                            S3: (H2, H2 + 1), OUT3: (S3, S3, S3 + 1, S3 + 1), K0: (X_T, X_T + 1)}.get(j)
                sources = None if by_chunk is None else (graph, by_chunk)
                if j < AX:
                    for t in range(NT):
                        last = pe.transpose(bank[:, t * P:(t + 1) * P],
                                            adj_in[:, t, j * P:(j + 1) * P], ident[:])
                elif j < H1:
                    if j == AX and part == 0:
                        pe.wait_ge(x_hi, due(graph, 1, 1))
                        pe.wait_ge(x_lo, due(graph, NT, NT))
                    f = j - AX
                    last = three(bank[:], lambda i, m: x_part[i][:, m, f * P:(f + 1) * P],
                                 lambda i, m: adjT[i][:, m, :], NT, part, PARTS[j], sources)
                elif j < S2:
                    f = j - H1
                    last = three(bank[:], lambda i, c: w_gcn[i][:, 0, c, f * P:(f + 1) * P],
                                 lambda i, c: axT_part[i][:, c, :], FC, sources=sources)
                elif j < H2 or S3 <= j < OUT3:
                    layer = 1 if j < H2 else 2
                    for t in range(2):
                        n = 2 * (j - (S2 if j < H2 else S3)) + t
                        last = three(bank[:, t * F:(t + 1) * F],
                                     lambda i, c: hids[i][:, c, n * P:(n + 1) * P],
                                     lambda i, c: w_gcn[i][:, layer, c, :], FC, sources=sources)
                elif j < S3:
                    f = j - H2
                    last = three(bank[:], lambda i, m: sup_part[i][:, m, f * P:(f + 1) * P],
                                 lambda i, m: adjT[i][:, m, :], NT, part, PARTS[j], sources)
                elif j < X_T:
                    n = 2 * (j - OUT3) + part
                    last = three(bank[:, part * F:(part + 1) * F],
                                 lambda i, m: adjT[i][:, m, n * P:(n + 1) * P],
                                 lambda i, m: sup_part[i][:, m, :], NT, sources=sources)
                elif j < K0:
                    if j == X_T:
                        pe.wait_ge(xn_ready, due(graph, NT, NT))
                    for t in range(NT):
                        last = pe.transpose(bank[:, t * P:(t + 1) * P],
                                            xn[:, t, (j - X_T) * P:(j - X_T + 1) * P], ident[:])
                elif j in (V, V + 1):
                    for t in range(2):
                        n = 2 * (j - V) + t
                        last = three(bank[:, t * F:(t + 1) * F],
                                     lambda i, c: xT_part[i][:, c, n * P:(n + 1) * P],
                                     lambda i, c: w_qkv[i][:, 2, c, :], FC)
                else:
                    g = 0 if j < V else 1
                    w = 0 if j in (Q0, Q1) else 1
                    last = three(bank[:], lambda i, c: w_qkv[i][:, w, c, g * P:(g + 1) * P],
                                 lambda i, c: xT_part[i][:, c, :], FC, sources=sources)
                if part == PARTS[j] - 1:
                    last.then_inc(job_made, 1)

            def scores(b, i):
                graph = (b, 0)
                if not exists(graph):
                    return
                step, h = divmod(i, GROUP)
                g, t = divmod(step, NT)
                if i % (SLOTS // GROUPS) == 0:
                    pe.wait_ge(stack_ready[g], due(graph, 16 * STACK_DMAS, 16 * STACK_DMAS))
                if (n := due(graph, SLOTS, i - 1)) is not None:
                    pe.wait_ge(masked_ready, n)
                head = GROUP * g + h
                pe.matmul(score_ps[i % 2][:], stack["q"][:, head, t * P:(t + 1) * P],
                          stack["k"][:, head, :], start=True, stop=True).then_inc(scores_made, 1)

            def turn(b, i):
                graph, k = ago(b, i, TRANSPOSE_LAG)
                if not exists(graph):
                    return
                pe.wait_ge(probs_ready, due(graph, SLOTS, k + 1))
                if (k - 2) % GROUP < ACT_COPIES:
                    if (n := due(graph, ACT_COPIES * STEPS, act_copies(k - 1))) is not None:
                        pe.wait_ge(copied_act, n)
                else:
                    if (n := due(graph, STEPS, (k - 1) // GROUP)) is not None:
                        pe.wait_ge(copied_dve, n)
                for c in range(NT):
                    last = pe.transpose(turn_ps[k % 2][:, c * P:(c + 1) * P],
                                        probs[:, k % 4, c * P:(c + 1) * P], ident[:])
                last.then_inc(turned, 1)

            def context(b, i):
                if (i - PV_LAG) % GROUP:
                    return
                graph, k = ago(b, i, PV_LAG)
                if not exists(graph):
                    return
                step = k // GROUP
                g, t = divmod(step, NT)
                pe.wait_ge(copied_act, due(graph, ACT_COPIES * STEPS, ACT_COPIES * (step + 1)))
                pe.wait_ge(copied_dve, due(graph, STEPS, step + 1))
                if t == 0:
                    pe.wait_ge(v_ready[g], due(graph, 16, 16))
                if (n := due(graph, STEPS, step)) is not None:
                    pe.wait_ge(ctx_ready, n)
                if (n := due(graph, NT, max(step - NT, 0))) is not None:
                    pe.wait_ge(y2_ready, n)
                for c in range(NT):
                    for h in range(GROUP):
                        col = g * P + DH * h
                        pe.matmul(ctx_acc[DH * h:DH * (h + 1), :], v_use[:, c, col:col + DH],
                                  probsT[:, step % 2, h, c * P:(c + 1) * P],
                                  start=(c == 0), stop=(c == NT - 1), tile_position=(0, DH * h))
                pe.wait_ge(rinv_ready, due(graph, STEPS, step + 1))
                pe.transpose(rinv_ps, rinv_wide[:], ident[:]).then_inc(pv_made, 1)

            def out_product(b, i):
                if (i - WO_LAG) % GROUP:
                    return
                graph, k = ago(b, i, WO_LAG)
                step = k // GROUP
                g, t = divmod(step, NT)
                if not exists(graph) or g != GROUPS - 1:
                    return
                pe.wait_ge(ctx_ready, due(graph, STEPS, step + 1))
                for e in range(FC):
                    last = pe.matmul(wo_ps, ctxT[:, e, t, :], w_o[:, e, :], start=(e == 0), stop=(e == FC - 1))
                last.then_inc(wo_made, 1)

            def iteration(b):
                for i in slots(b):
                    scores(b, i)
                    turn(b, i)
                    context(b, i)
                    out_product(b, i)
                    for j, part in PLAN.get(i, []):
                        job(b, j, part)

            pe.wait_ge(w_ready, 9)
            iterations(pe, iteration, B - 2)

        @block.scalar
        def _(act):
            def copy_turned(b, i):
                graph, k = ago(b, i, TRANSPOSE_LAG)
                step, h = divmod(k, GROUP)
                if not exists(graph) or h >= ACT_COPIES:
                    return
                act.wait_ge(turned, due(graph, SLOTS, k + 1))
                if (n := due(graph, STEPS, step - 1)) is not None:
                    act.wait_ge(pv_made, n)
                act.activation(probsT[:, step % 2, h, :], turn_ps[k % 2][:], ACT.Copy).then_inc(copied_act, 1)

            def exponentials(b, i):
                graph, k = ago(b, i, EXP_LAG)
                if not exists(graph):
                    return
                step, h = divmod(k, GROUP)
                act.wait_ge(shift_ready, due(graph, SLOTS, k + 1))
                if (n := due(graph, SLOTS, k - 3)) is not None:
                    act.wait_ge(turned, n)
                if h == 0 and (n := due(graph, STEPS, step - 1)) is not None:
                    act.wait_ge(rinv_raw, n)
                act.activation(probs[:, k % 4, :], masked[:, k % 2, :], ACT.Exp, bias=shift[:, h:h + 1],
                               scale=SCORE_SCALE, accum_out=rowsum[:, step % 2, h:h + 1]).then_inc(probs_ready, 1)

            def job(b, j):
                graph = (b, 1)
                if not exists(graph) or j in VECTOR_ONLY:
                    return
                bank = job_ps[j % JOB_BANKS][:]
                act.wait_ge(job_made, due(graph, JOBS, j + 1))
                if j in RELU_JOBS:
                    layer, f = (0, j - H1) if j < S2 else (1, j - H2)
                    if (n := due(graph, JOBS, S2 if layer else H2 + 2 - JOBS)) is not None:
                        act.wait_ge(job_done, n)
                    act.activation(hid[:, f, :], bank, ACT.Relu, bias=b_cols[:, layer, f:f + 1]).then_inc(job_hi, 1)
                elif j in (K0, Q0, K1, Q1):
                    g = 0 if j < V else 1
                    t = "q" if j in (Q0, Q1) else "k"
                    if (n := due(graph, 16 * STACK_DMAS, 0)) is not None:
                        act.wait_ge(stack_ready[g], n)
                    act.activation(qk[t][0][:, g, :], bank, ACT.Identity,
                                   bias=b_cols[:, 2 + (t == "k"), g:g + 1]).then_inc(job_hi, 1)
                else:
                    act.activation(split_target(j)[0], bank, ACT.Copy).then_inc(job_hi, 1)

            def iteration(b):
                for i in slots(b):
                    copy_turned(b, i)
                    exponentials(b, i)
                    for j in jobs_in(i):
                        job(b, j)

            act.wait_ge(w_ready, 9)
            iterations(act, iteration, B - 2)

        @block.vector
        def _(dve):
            dve.wait_ge(w_loaded, 16 * 14)
            dve.tensor_copy(b_by_feature.rearrange("n (d h) -> n d h", h=GROUP),
                            b_staged[:, 1, :].rearrange("n (h d) -> n d h", h=GROUP)).then_inc(b_ordered, 1)
            dve.tensor_copy(w_gcn[0][:], staged[:, 0:3, :, :]).then_inc(w_hi, 1)
            dve.wait_ge(w_hi, 1)
            dve.tensor_tensor(w_gcn[1][:], staged[:, 0:3, :, :], w_gcn[0][:].bitcast(F32),
                              ALU.subtract).then_inc(w_ready, 1)
            for n, bank in enumerate((*job_ps, score_ps[0])):
                turned_w = bank[:].rearrange("p (e f) -> p e f", e=FC)
                dve.wait_ge(w_turned, n + 1)
                for e in range(FC if n < 3 else 0):
                    split = "(g h d) -> g d h" if n < 2 else "(g h d) -> g h d"
                    hi, lo = (w_qkv[i][:, n, e, :].rearrange("p (g a b) -> p g a b", g=GROUPS,
                                                             a=DH if n < 2 else GROUP) for i in range(2))
                    src = turned_w[:, e, :].rearrange(f"p {split}".replace("-> ", "-> p "), g=GROUPS, h=GROUP)
                    dve.tensor_copy(hi, src).then_inc(w_hi, 1)
                    dve.wait_ge(w_hi, FC * n + e + 2)
                    dve.tensor_tensor(lo, src, hi.bitcast(F32), ALU.subtract).then_inc(w_ready, 1)
                if n == 3:
                    dve.tensor_copy(w_o[:], turned_w).then_inc(w_ready, 1)

            dve.wait_ge(w_turned, 5)
            dve.tensor_copy(b_cols[:].rearrange("p n c -> p (n c)"), score_ps[1][:, 0:4 * FC]).then_inc(w_ready, 1)

            def mask_scores(b, i):
                graph = (b, 0)
                if not exists(graph):
                    return
                t = i // GROUP % NT
                made = held(dve, due(graph, SLOTS, i + 1))
                used = held(dve, due(graph, SLOTS, i - 1))
                loaded = held(dve, due(graph, 16, 16))
                dve.wait_ge(ident_ready, 1)
                dve.wait_ge(scores_made, made)
                if used is not None:
                    dve.wait_ge(probs_ready, used)
                if i % GROUP == 0 and i < SLOTS // GROUPS:
                    dve.wait_ge(mask_loaded[t], loaded)
                dve.tensor_tensor_reduce(masked[:, i % 2, :], score_ps[i % 2][:], mask[:, t, :], 1.0,
                                         float(np.finfo(np.float32).min), ALU.mult, ALU.max,
                                         rowmax[:, i % GROUP:i % GROUP + 1]).then_inc(masked_ready, 1)

            def copy_turned(b, i):
                graph, k = ago(b, i, TRANSPOSE_LAG)
                step, h = divmod(k, GROUP)
                if not exists(graph) or h < ACT_COPIES:
                    return
                dve.wait_ge(turned, due(graph, SLOTS, k + 1))
                if (n := due(graph, STEPS, step - 1)) is not None:
                    dve.wait_ge(pv_made, n)
                dve.tensor_copy(probsT[:, step % 2, h, :], turn_ps[k % 2][:]).then_inc(copied_dve, 1)

            def reciprocals(b, i):
                if (i - RINV_LAG) % GROUP:
                    return
                graph, k = ago(b, i, RINV_LAG)
                if not exists(graph):
                    return
                step = k // GROUP
                dve.wait_ge(probs_ready, due(graph, SLOTS, GROUP * (step + 1)))
                dve.reciprocal(rinv[:, step % 2, :], rowsum[:, step % 2, :]).then_inc(rinv_raw, 1)
                dve.wait_ge(rinv_raw, due(graph, STEPS, step + 1))
                if (n := due(graph, STEPS, step)) is not None:
                    dve.wait_ge(pv_made, n)
                dve.tensor_copy(rinv_wide[:].rearrange("p (h d) -> p h d", h=GROUP),
                                rinv[:, step % 2, :].unsqueeze(2).to_broadcast([P, GROUP, DH]))\
                    .then_inc(rinv_ready, 1)

            def normalise_context(b, i):
                if (i - CTX_LAG) % GROUP:
                    return
                graph, k = ago(b, i, CTX_LAG)
                if not exists(graph):
                    return
                step = k // GROUP
                g, t = divmod(step, NT)
                dve.wait_ge(pv_made, due(graph, STEPS, step + 1))
                dve.tensor_copy(rinvT[:], rinv_ps).then_inc(rinvT_ready, 1)
                dve.wait_ge(rinvT_ready, due(graph, STEPS, step + 1))
                dve.tensor_tensor(ctxT[:, g, t, :], ctx_acc, rinvT[:], ALU.mult).then_inc(ctx_ready, 1)

            def residual2(b, i):
                if (i - Y2_LAG) % GROUP:
                    return
                graph, k = ago(b, i, Y2_LAG)
                g, t = divmod(k // GROUP, NT)
                if not exists(graph) or g != GROUPS - 1:
                    return
                dve.wait_ge(wo_made, due(graph, NT, t + 1))
                dve.wait_ge(res_ready, due(graph, NT, NT))
                dve.tensor_tensor(y2[:, t % 2, :], wo_ps, res[:, t, :], ALU.add).then_inc(y2_ready, 1)

            def moments2(b, i):
                if (i - STATS2_LAG) % GROUP:
                    return
                graph, k = ago(b, i, STATS2_LAG)
                g, t = divmod(k // GROUP, NT)
                if not exists(graph) or g != GROUPS - 1:
                    return
                dve.wait_ge(y2_ready, due(graph, NT, t + 1))
                dve.bn_stats(stats2[:, t % 2, :], y2[:, t % 2, :]).then_inc(stats2_ready, 1)
                n = held(dve, due(graph, NT, t + 1))
                dve.wait_ge(ident_ready, 1)
                dve.wait_ge(stats2_ready, n)
                dve.bn_aggr(mv2[:, t % 2, :], stats2[:, t % 2, :]).then_inc(mv2_ready, 1)

            def normalise2(b, i):
                if (i - NORM2_LAG) % GROUP:
                    return
                graph, k = ago(b, i, NORM2_LAG)
                g, t = divmod(k // GROUP, NT)
                if not exists(graph) or g != GROUPS - 1:
                    return
                dve.wait_ge(rstd2_ready, due(graph, NT, t + 1))
                if (n := due(graph, 16 * NT // 2, 16 * (t // 2))) is not None:
                    dve.wait_ge(out_stored[t % 2], n)
                dve.tensor_scalar(out_sb[:, t % 2, :], y2[:, t % 2, :], mv2[:, t % 2, 0:1], rstd2[:, t % 2, 0:1],
                                  ALU.subtract, ALU.mult).then_inc(out_ready, 1)

            def split_x(b):
                graph = (b, 1)
                if exists(graph):
                    dve.wait_ge(x_loaded, due(graph, 16, 16))
                    if (n := due(graph, JOBS, 0)) is not None:
                        dve.wait_ge(job_made, n)
                    dve.tensor_copy(xs[0][:], x_in[:].rearrange("p t f -> p (t f)")).then_inc(x_hi, 1)

            def job(b, j):
                graph = (b, 1)
                if not exists(graph):
                    return
                bank = job_ps[j % JOB_BANKS][:]
                if j in VECTOR_ONLY:
                    dve.wait_ge(job_made, due(graph, JOBS, j + 1))
                else:
                    dve.wait_ge(job_hi, due(graph, len(SCALAR_JOBS), scalar_count(j)))
                if j in RELU_JOBS:
                    f = j - (H1 if j < S2 else H2)
                    order = (H1, H1 + 1, H2, H2 + 1).index(j)
                    dve.tensor_copy(hids[0][:, f, :], hid[:, f, :]).then_inc(hid_hi, 1)
                    dve.wait_ge(hid_hi, due(graph, len(RELU_JOBS), order + 1))
                    dve.tensor_tensor(hids[1][:, f, :], hid[:, f, :], hids[0][:, f, :].bitcast(F32),
                                      ALU.subtract).then_inc(job_done, 1)
                elif j in (K0, Q0, K1, Q1):
                    g = 0 if j < V else 1
                    t = "q" if j in (Q0, Q1) else "k"
                    dve.scalar_tensor_tensor(out=qk[t][1][:, g, :], in0=bank,
                                             scalar=b_cols[:, 2 + (t == "k"), g:g + 1],
                                             in1=qk[t][0][:, g, :].bitcast(F32),
                                             op0=ALU.add, op1=ALU.subtract).then_inc(job_done, 1)
                elif j in (V, V + 1):
                    for g in range(GROUPS):
                        if (n := due(graph, 16, 0)) is not None:
                            dve.wait_ge(v_ready[g], n)
                    n = 2 * (j - V)
                    dve.tensor_tensor(v_new[:, n:n + 2, :], bank.rearrange("p (t f) -> p t f", t=2),
                                      b_rows[:, 1:2, :].to_broadcast([P, 2, F]), ALU.add).then_inc(job_done, 1)
                elif j in (OUT3, OUT3 + 1):
                    a = j - OUT3
                    dve.wait_ge(xb_ready, due(graph, NT, 2 * a + 2))
                    dve.tensor_tensor(y1[:, a, :, :], bank.rearrange("p (t f) -> p t f", t=2),
                                      xb[:, 2 * a:2 * a + 2, :], ALU.add).then_inc(job_done, 1)
                else:
                    hi, lo = split_target(j)
                    dve.tensor_tensor(lo, bank, hi.bitcast(F32), ALU.subtract).then_inc(job_done, 1)

            def moments1(b, a):
                graph = (b, 1)
                if exists(graph):
                    dve.wait_ge(job_done, due(graph, JOBS, OUT3 + a + 1))
                    for t in range(2):
                        dve.bn_stats(stats1[:, a, t, :], y1[:, a, t, :]).then_inc(stats1_ready, 1)
                    for t in range(2):
                        n = held(dve, due(graph, NT, 2 * a + t + 1))
                        dve.wait_ge(ident_ready, 1)
                        dve.wait_ge(stats1_ready, n)
                        dve.bn_aggr(mv1[:, a, t, :], stats1[:, a, t, :]).then_inc(mv1_ready, 1)

            def normalise1(b, a):
                graph = (b, 1)
                if not exists(graph):
                    return
                dve.wait_ge(rstd1_ready, due(graph, 2, a + 1))
                if (n := due(graph, NT, 0)) is not None:
                    dve.wait_ge(res_ready, n)
                for t in range(2):
                    dve.tensor_scalar(xn[:, 2 * a + t, :], y1[:, a, t, :], mv1[:, a, t, 0:1],
                                      rstd1[:, a, t:t + 1], ALU.subtract, ALU.mult).then_inc(xn_ready, 1)

            def iteration(b):
                for i in slots(b):
                    mask_scores(b, i)
                    if i == 0:
                        split_x(b)
                    copy_turned(b, i)
                    reciprocals(b, i)
                    normalise_context(b, i)
                    residual2(b, i)
                    for j in jobs_in(i):
                        job(b, j)
                    for a in range(2):
                        if OUT3 + a in jobs_in(i - STATS1_LAG):
                            moments1(b, a)
                        if OUT3 + a in jobs_in(i - NORM1_LAG):
                            normalise1(b, a)
                    moments2(b, i)
                    normalise2(b, i)

            iterations(dve, iteration, B - 2)

        @block.gpsimd
        def _(pool):
            pool.memset(ident[:], 0.0).then_inc(ident_zero, 1)
            pool.memset(minus_half[:], -0.5).then_inc(ident_zero, 1)
            pool.wait_ge(ident_zero, 2)
            pool.affine_select(out=ident[:], in_=ident[:], compare_op=ALU.not_equal, fill=1.0, base=0,
                               pattern=[[-1, P]], channel_multiplier=1).then_inc(ident_ready, 1)

            def shifts(b, i):
                graph = (b, 0)
                if exists(graph):
                    h = i % GROUP
                    n = held(pool, due(graph, SLOTS, i + 1))
                    pool.wait_ge(ident_ready, 1)
                    pool.wait_ge(masked_ready, n)
                    pool.tensor_scalar(shift[:, h:h + 1], rowmax[:, h:h + 1], -SCORE_SCALE, None,
                                       ALU.mult).then_inc(shift_ready, 1)

            def lo_of_x(b, t):
                graph = (b, 1)
                if exists(graph):
                    pool.wait_ge(x_hi, due(graph, 1, 1))
                    cols = slice(t * F, (t + 1) * F)
                    pool.tensor_tensor(xs[1][:, cols], x_in[:, t, :], xs[0][:, cols].bitcast(F32),
                                       ALU.subtract).then_inc(x_lo, 1)

            def x_with_bias(b, t):
                graph = (b, 1)
                if exists(graph):
                    if (n := due(graph, JOBS, OUT3 + 2 - JOBS)) is not None:
                        pool.wait_ge(job_done, n)
                    pool.tensor_tensor(xb[:, t, :], x_in[:, t, :], b_rows[:, 0, :], ALU.add).then_inc(xb_ready, 1)

            def residual(b, t):
                graph = (b, 0)
                if exists(graph):
                    pool.wait_ge(xn_ready, due(graph, NT, NT))
                    if (n := due(graph, NT, 0)) is not None:
                        pool.wait_ge(y2_ready, n)
                    pool.tensor_tensor(res[:, t, :], xn[:, t, :], b_rows[:, 2, :], ALU.add).then_inc(res_ready, 1)

            def rstd_1(b, a):
                graph = (b, 1)
                if exists(graph):
                    n = held(pool, due(graph, NT, 2 * a + 2))
                    pool.wait_ge(ident_ready, 1)
                    pool.wait_ge(mv1_ready, n)
                    pool.tensor_scalar(ve1[:, a, :], mv1[:, a, :, 1], EPS, None, ALU.add).then_inc(ve1_ready, 1)
                    pool.wait_ge(ve1_ready, due(graph, 2, a + 1))
                    pool.tensor_tensor(rstd1[:, a, :], ve1[:, a, :], minus_half[:], ALU.pow).then_inc(rstd1_ready, 1)

            def rstd_2(b, i):
                if (i - STATS2_LAG) % GROUP:
                    return
                graph, k = ago(b, i, STATS2_LAG)
                g, t = divmod(k // GROUP, NT)
                if not exists(graph) or g != GROUPS - 1:
                    return
                n = held(pool, due(graph, NT, t + 1))
                pool.wait_ge(ident_ready, 1)
                pool.wait_ge(mv2_ready, n)
                pool.tensor_scalar(ve2[:, t % 2, :], mv2[:, t % 2, 1:2], EPS, None, ALU.add).then_inc(ve2_ready, 1)
                pool.wait_ge(ve2_ready, due(graph, NT, t + 1))
                pool.tensor_tensor(rstd2[:, t % 2, :], ve2[:, t % 2, :], minus_half[:, 0:1],
                                   ALU.pow).then_inc(rstd2_ready, 1)

            def iteration(b):
                for i in slots(b):
                    shifts(b, i)
                    rstd_2(b, i)
                    if i < 2:
                        lo_of_x(b, 2 * i)
                        lo_of_x(b, 2 * i + 1)
                    elif 4 <= i < 8:
                        x_with_bias(b, i - 4)
                    elif 9 <= i < 13:
                        residual(b, i - 9)
                    for a in range(2):
                        if OUT3 + a in jobs_in(i - STATS1_LAG):
                            rstd_1(b, a)

            pool.wait_ge(w_loaded, 16 * 14)
            iterations(pool, iteration, B - 2)


_INS = ["x", "adj", "L0_gnn_W1", "L0_gnn_b1", "L0_gnn_W2", "L0_gnn_b2", "L0_gnn_W3", "L0_gnn_b3",
        "L1_gnn_Wq", "L1_gnn_bq", "L1_gnn_Wk", "L1_gnn_bk", "L1_gnn_Wv", "L1_gnn_bv", "L1_gnn_Wo", "L1_gnn_bo"]


def kernel(**inputs):
    import concourse.bacc as _bacc
    from concourse.bass_utils import run_bass_kernel_spmd as _run

    nc = _bacc.Bacc("TRN2", target_bir_lowering=False, num_devices=1)
    arrays, args = {}, []
    for name in _INS:
        a = np.ascontiguousarray(inputs[name])
        arrays[f"in_{name}"] = a
        args.append(nc.dram_tensor(f"in_{name}", a.shape, mybir.dt.from_np(a.dtype), kind="ExternalInput").ap())
    out = nc.dram_tensor("out", inputs["x"].shape, F32, kind="ExternalOutput").ap()
    gcn_attention_kernel(nc, *args, out)
    r = _run(nc, [arrays], core_ids=[0])
    return r.results[0]["out"]
```

```python
from contextlib import ExitStack

import numpy as np

import concourse.bass as bass
from concourse import mybir

F32 = mybir.dt.float32
F32R = mybir.dt.float32r
ALU = mybir.AluOpType
ACT = mybir.ActivationFunctionType

P = 128
HEADS = 8
EPS = 1e-5

ADJ_T, AX, H1, S2, H2, S3, OUT3, X_T, K0, Q0, V, K1, Q1 = 0, 4, 6, 8, 10, 12, 14, 18, 20, 21, 22, 24, 25
JOBS = 26
JOB_BANKS = 3
BANK = [(j + (j >= X_T)) % JOB_BANKS for j in range(JOBS)]
PARTS = [2 if j in (AX, AX + 1, H2, H2 + 1) else 1 for j in range(JOBS)]
PLAN = {
    0: [(0, 0), (1, 0)], 1: [(2, 0), (3, 0)],
    2: [(AX, 0)], 3: [(AX, 1)], 5: [(AX + 1, 0)], 6: [(AX + 1, 1)],
    7: [(H1, 0)], 8: [(H1 + 1, 0)],
    10: [(S2, 0)], 11: [(S2 + 1, 0)],
    12: [(H2, 0)], 14: [(H2, 1)], 15: [(H2 + 1, 0)], 16: [(H2 + 1, 1)],
    17: [(S3, 0)], 18: [(S3 + 1, 0)],
    20: [(OUT3, 0)], 21: [(OUT3 + 1, 0)], 22: [(OUT3 + 2, 0)], 23: [(OUT3 + 3, 0)],
    25: [(X_T, 0), (X_T + 1, 0)],
    26: [(K0, 0)], 27: [(Q0, 0)], 28: [(V, 0)], 29: [(V + 1, 0)], 30: [(K1, 0)], 31: [(Q1, 0)],
}
assert [x for i in sorted(PLAN) for x in PLAN[i]] == [(j, k) for j in range(JOBS) for k in range(PARTS[j])]
RELU_JOBS = (H1, H1 + 1, H2, H2 + 1)
VECTOR_ONLY = (*range(OUT3, X_T), V, V + 1)
SCALAR_JOBS = [j for j in range(JOBS) if j not in VECTOR_ONLY]

EXP_LAG, TRANSPOSE_LAG = 1, 4
RINV_LAG, PV_LAG, CTX_LAG, WO_LAG, Y2_LAG, STATS2_LAG, NORM2_LAG = 7, 9, 9, 10, 11, 12, 13
NORM1_LAG = 1
SPLIT_X_SLOTS, LO_OF_X_SLOTS = (9, 13), (11, 14, 17, 18)
RESIDUAL_SLOTS, X_WITH_BIAS_SLOTS = (6, 10, 12, 15), (25, 26, 27, 29)
QKVO = ((1, 7, 12), (0, 10, 15), (2, 25, 26), (3, 25, 27))
GCN_SLOT, BIAS_SLOT = 1, 3
DRAIN_SLOTS = NORM2_LAG - 3


def gcn_attention_kernel(nc, x, adj, W1, b1, W2, b2, W3, b3, Wq, bq, Wk, bk, Wv, bv, Wo, bo, out):
    B, N, F = x.shape
    NT, FC = N // P, F // P
    DH = F // HEADS
    GROUP = P // DH
    GROUPS = HEADS // GROUP
    SLOTS = HEADS * NT
    STEPS = SLOTS // GROUP
    TERMS = P // DH
    assert (NT, FC, DH, GROUP, GROUPS, TERMS) == (4, 2, 32, 4, 2, 4)
    SCORE_SCALE = 2.0 * DH ** -0.5
    STACK_DMAS = 2 * TERMS
    MASKED = 4
    VECTOR_HEAD, ACT_COPIES = 2, GROUP - 1

    x_v = x.rearrange("b (t p) f -> b p t f", p=P)
    adj_v = adj.rearrange("b (t p) m -> b p t m", p=P)
    out_v = out.rearrange("b (t p) f -> b p t f", p=P)

    with ExitStack() as ctx:
        def sb(name, shape, dt=F32):
            return ctx.enter_context(nc.sbuf_tensor(name, shape, dt))

        def sem(name):
            return ctx.enter_context(nc.semaphore(name))

        ident = sb("ident", [P, P])
        adj_in = sb("adj_in", [P, NT, N])
        mask = sb("mask", [P, NT, N])
        adjT = [sb(f"adjT_{k}", [P, NT, N], F32R) for k in "hl"]
        x_in = sb("x_in", [P, NT, F])
        xs = [sb(f"xs_{k}", [P, NT, F], F32R) for k in "hl"]
        xb = sb("xb", [P, NT, F])
        prod = [sb(f"prod_{k}", [P, NT * F], F32R) for k in "hl"]
        hid = sb("hid", [P, FC, N])
        hids = [sb(f"hids_{k}", [P, FC, N], F32R) for k in "hl"]
        y1 = sb("y1", [P, 2, 2, F])
        xn = sb("xn", [P, NT, F])
        res = sb("res", [P, NT, F])
        qk = {t: [sb(f"{t}_{k}", [P, GROUPS, N], F32R) for k in "hl"] for t in "qk"}
        stack = {t: sb(f"{t}_stack", [P, HEADS, N], F32R) for t in "qk"}
        v_new = sb("v_new", [P, NT, F])
        v_use = sb("v_use", [P, NT, F])
        masked = sb("masked", [P, MASKED, N])
        probs = sb("probs", [P, 4, N])
        probsT = sb("probsT", [P, 2, GROUP, N])
        ctxT = sb("ctxT", [P, GROUPS, NT, P])
        rinvT = sb("rinvT", [P, P])
        y2 = sb("y2", [P, 2, F])
        out_sb = sb("out_sb", [P, 2, F])
        w_gcn = [sb(f"w_gcn_{k}", [P, 3, FC, F], F32R) for k in "hl"]
        w_qkv = [sb(f"w_qkv_{k}", [P, 3, FC, F], F32R) for k in "hl"]
        w_o = sb("w_o", [P, FC, F])
        b_cols = sb("b_cols", [P, 4, FC])
        b_rows = sb("b_rows", [P, 3, F])
        rowmax = sb("rowmax", [P, GROUP])
        shift = sb("shift", [P, GROUP])
        rowsum = sb("rowsum", [P, 2, GROUP])
        rinv = sb("rinv", [P, 2, GROUP])
        rinv_wide = sb("rinv_wide", [P, P])
        stats1 = sb("stats1", [P, 2, 2, 6])
        mv1 = sb("mv1", [P, 2, 2, 2])
        ve1 = sb("ve1", [P, 2, 2])
        rstd1 = sb("rstd1", [P, 2, 2])
        stats2 = sb("stats2", [P, 2, 6])
        mv2 = sb("mv2", [P, 2, 2])
        ve2 = sb("ve2", [P, 2, 1])
        rstd2 = sb("rstd2", [P, 2, 1])
        minus_half = sb("minus_half", [P, 2])
        staged = probsT[:, :, :, :].rearrange("p a h n -> p (a h n)")[:, 0:7 * FC * F]\
            .rearrange("p (w c f) -> p w c f", w=7, c=FC)

        b_staged = masked[0:2 * FC, :, 0:P]
        b_by_feature = masked[0:2 * FC, 0, P:2 * P]

        def ps(name):
            return ctx.enter_context(nc.psum_tensor(name, [P, N], F32))

        score_ps = [ps("score0"), ps("score1")]
        turn_ps = [ps("turn0"), ps("turn1")]
        ctx_ps = ps("ctx_ps")
        ctx_acc, rinv_ps, wo_ps = ctx_ps[:, 0:P], ctx_ps[:, P:2 * P], ctx_ps[:, 2 * P:2 * P + F]
        job_ps = [ps(f"job{k}") for k in range(JOB_BANKS)]

        w_ps, b_ps = (score_ps[0], turn_ps[0], turn_ps[1], ctx_ps), score_ps[1]

        gcn_loaded, b_loaded, w_loaded = sem("gcn_loaded"), sem("b_loaded"), sem("w_loaded")
        ident_zero, ident_ready = sem("ident_zero"), sem("ident_ready")
        gcn_hi, gcn_ready = sem("gcn_hi"), sem("gcn_ready")
        b_ordered, b_turned, b_ready = sem("b_ordered"), sem("b_turned"), sem("b_ready")
        w_turned, w_hi, w_ready = sem("w_turned"), sem("w_hi"), sem("w_ready")
        x_loaded, adj_loaded = sem("x_loaded"), sem("adj_loaded")
        mask_loaded = [sem(f"mask_loaded{t}") for t in range(NT)]
        stack_ready = [sem(f"stack_ready{g}") for g in range(GROUPS)]
        v_ready = [sem(f"v_ready{g}") for g in range(GROUPS)]
        out_stored = [sem(f"out_stored{k}") for k in range(2)]
        x_hi, x_lo, xb_ready, res_ready = sem("x_hi"), sem("x_lo"), sem("xb_ready"), sem("res_ready")
        job_made, job_hi, job_done = sem("job_made"), sem("job_hi"), sem("job_done")
        hid_hi = sem("hid_hi")
        stats1_ready, mv1_ready = sem("stats1_ready"), sem("mv1_ready")
        ve1_ready, rstd1_ready, xn_ready = sem("ve1_ready"), sem("rstd1_ready"), sem("xn_ready")
        scores_made, masked_ready, shift_ready = sem("scores_made"), sem("masked_ready"), sem("shift_ready")
        probs_ready, turned = sem("probs_ready"), sem("turned")
        copied_act, copied_dve = sem("copied_act"), sem("copied_dve")
        rinv_raw, rinv_ready, pv_made, rinvT_ready, ctx_ready = (
            sem("rinv_raw"), sem("rinv_ready"), sem("pv_made"), sem("rinvT_ready"), sem("ctx_ready"))
        wo_made, y2_ready, stats2_ready, mv2_ready = (
            sem("wo_made"), sem("y2_ready"), sem("stats2_ready"), sem("mv2_ready"))
        ve2_ready, rstd2_ready, out_ready = sem("ve2_ready"), sem("rstd2_ready"), sem("out_ready")

        def exists(graph):
            b, off = graph
            return not isinstance(b, int) or 0 <= b + off < B

        def due(graph, per_graph, count):
            b, off = graph
            n = b * per_graph + (off * per_graph + count)
            return None if isinstance(n, int) and n <= 0 else n

        def held(eng, value):
            return eng.to_reg(value) if value is not None and not isinstance(value, int) else value

        def ago(b, slot, lag):
            return ((b, 0), slot - lag) if slot >= lag else ((b, -1), slot - lag + SLOTS)

        def iterations(eng, iteration, last_looped):
            iteration(-1)
            iteration(0)
            with eng.Fori(1, last_looped + 1) as b:
                iteration(b)
            for b in range(last_looped + 1, B):
                iteration(b)
            iteration(B)

        def starting(b):
            return isinstance(b, int) and b == -1

        def slots(b):
            return range(DRAIN_SLOTS if isinstance(b, int) and b == B else SLOTS)

        def jobs_in(slot):
            return [j for j, part in PLAN.get(slot, []) if part == PARTS[j] - 1]

        def last_in_bank(j):
            return max(k if k < j else k - JOBS for k in range(JOBS) if k != j and BANK[k] == BANK[j])

        def scalar_count(j):
            return sum(k <= j for k in SCALAR_JOBS)

        def act_copies(slot):
            return slot - vector_copies(slot)

        def vector_copies(slot):
            return (slot - VECTOR_HEAD + GROUP - 1) // GROUP

        def split_target(j):
            if j < AX:
                return [t[:, j, :] for t in adjT]
            if j < H1:
                return [t[:, (j - AX) * N:(j - AX + 1) * N] for t in prod]
            if S2 <= j < H2:
                return [t[:, (j - S2) * N:(j - S2 + 1) * N] for t in prod]
            if S3 <= j < OUT3:
                return [t[:, (j - S3) * N:(j - S3 + 1) * N] for t in prod]
            if X_T <= j < K0:
                return [t[:, j - X_T, :] for t in hids]
            raise ValueError(j)

        block = ctx.enter_context(nc.Block())

        @block.sync
        def _(sp):
            sp.dma_start(x_in[:], x_v[0]).then_inc(x_loaded, 16)
            sp.dma_start(adj_in[:], adj_v[0]).then_inc(adj_loaded, 16)
            for n, w in enumerate((W1, W2, W3)):
                sp.dma_start(staged[:, n, :, :], w.rearrange("(c p) f -> p c f", p=P)).then_inc(gcn_loaded, 16)
            for n, v in enumerate((b1, b2, bq, bk)):
                sp.dma_start(b_staged[FC * (n % 2):FC * (n % 2 + 1), n // 2, :], v.rearrange("(c p) -> c p", p=P)).then_inc(b_loaded, 16)
            for n, v in enumerate((b3, bv, bo)):
                sp.dma_start(b_rows[:, n, :], v.partition_broadcast(P)).then_inc(b_loaded, 16)
            for n, w in enumerate((Wq, Wk, Wv, Wo)):
                sp.dma_start(staged[:, 3 + n, :, :], w.rearrange("(c p) f -> p c f", p=P)).then_inc(w_loaded, 16)

            def load_adj(b):
                if exists((b, 2)):
                    n = held(sp, due((b, 1), JOBS, ADJ_T + NT))
                    sp.wait_ge(ident_ready, 1)
                    sp.wait_ge(job_made, n)
                    sp.dma_start(adj_in[:], adj_v[b + 2]).then_inc(adj_loaded, 16)

            def load_x(b):
                if exists((b, 3)):
                    for used in (x_lo, xb_ready):
                        n = held(sp, due((b, 2), NT, NT))
                        sp.wait_ge(ident_ready, 1)
                        sp.wait_ge(used, n)
                    sp.dma_start(x_in[:], x_v[b + 3]).then_inc(x_loaded, 16)

            def load_mask(b, t):
                if exists((b, 1)):
                    if (n := held(sp, due((b, 0), SLOTS, SLOTS - (NT - 1 - t) * GROUP))) is not None:
                        sp.wait_ge(ident_ready, 1)
                        sp.wait_ge(masked_ready, n)
                    sp.dma_start(mask[:, t, :], adj_v[b + 1, :, t, :]).then_inc(mask_loaded[t], 16)

            def stack_group(b, g, t):
                if exists((b, 1)):
                    n = held(sp, due((b, 1), JOBS, {"k": (K0, K1), "q": (Q0, Q1)}[t][g] + 1))
                    sp.wait_ge(ident_ready, 1)
                    sp.wait_ge(job_done, n)
                    if (n := held(sp, due((b, 0), SLOTS, SLOTS // GROUPS * (g + 1)))) is not None:
                        sp.wait_ge(ident_ready, 1)
                        sp.wait_ge(scores_made, n)
                    for term in range(TERMS):
                        part = qk[t][term % 2 if t == "q" else term // 2]
                        sp.dma_start(
                            stack[t][DH * term:DH * (term + 1), GROUP * g:GROUP * (g + 1), :].bitcast(F32),
                            part[:, g, :].bitcast(F32)).then_inc(stack_ready[g], 16)

            def copy_v(b, g):
                if exists((b, 1)):
                    n = held(sp, due((b, 1), JOBS, V + 2))
                    sp.wait_ge(ident_ready, 1)
                    sp.wait_ge(job_done, n)
                    if (n := held(sp, due((b, 0), STEPS, NT * (g + 1)))) is not None:
                        sp.wait_ge(ident_ready, 1)
                        sp.wait_ge(pv_made, n)
                    cols = slice(g * P, (g + 1) * P)
                    sp.dma_start(v_use[:, :, cols], v_new[:, :, cols]).then_inc(v_ready[g], 16)

            def store(graph, t):
                if exists(graph):
                    b, off = graph
                    n = held(sp, due(graph, NT, t + 1))
                    sp.wait_ge(ident_ready, 1)
                    sp.wait_ge(out_ready, n)
                    sp.dma_start(out_v[b + off, :, t, :], out_sb[:, t % 2, :]).then_inc(out_stored[t % 2], 16)

            def iteration(b):
                load_mask_of_previous = not isinstance(b, int) or b >= 0
                if load_mask_of_previous:
                    stack_group(b - 1, 1, "k")
                    store((b, -1), 1)
                    stack_group(b - 1, 1, "q")
                    load_mask(b - 1, NT - 1)
                    store((b, -1), 2)
                load_adj(b)
                if load_mask_of_previous:
                    copy_v(b - 1, 1)
                    store((b, -1), 3)
                if isinstance(b, int) and b == B:
                    return
                load_mask(b, 0)
                load_mask(b, 1)
                stack_group(b, 0, "k")
                stack_group(b, 0, "q")
                load_mask(b, 2)
                store((b, 0), 0)
                copy_v(b, 0)
                load_x(b)

            load_x(-2)
            iterations(sp, iteration, B - 4)
            for k in range(2):
                n = held(sp, due((B - 1, 0), 16 * NT // 2, 16 * NT // 2))
                sp.wait_ge(ident_ready, 1)
                sp.wait_ge(out_stored[k], n)

        @block.tensor
        def _(pe):
            def three(dst, lhs, rhs, chunks, part=0, parts=1, sources=None):
                for c in range(chunks // parts * part, chunks // parts * (part + 1)):
                    if sources is not None:
                        graph, of_chunk = sources
                        pe.wait_ge(job_done, due(graph, JOBS, of_chunk[c] + 1))
                    for i, j in ((0, 0), (0, 1), (1, 0)):
                        last = pe.matmul(dst, lhs(i, c), rhs(j, c), start=(c == 0 and i + j == 0),
                                         stop=(c == chunks - 1 and i == 1))
                return last

            axT_part = [t[:].rearrange("p (c n) -> p c n", c=FC) for t in prod]
            sup_part = [t[:].rearrange("p (t f) -> p t f", t=NT) for t in prod]

            def turn_weights(n, w):
                pe.wait_ge(w_loaded, 16 * 4)
                for e in range(FC):
                    for c in range(FC):
                        last = pe.transpose(w_ps[n][:, (FC * e + c) * P:(FC * e + c + 1) * P],
                                            staged[:, 3 + w, c, e * P:(e + 1) * P], ident[:])
                last.then_inc(w_turned, 1)

            def turn_biases():
                pe.wait_ge(b_loaded, 16 * 7)
                pe.transpose(b_ps[:, 0:2 * FC], b_staged[:, 0, :], ident[0:2 * FC, 0:2 * FC])
                pe.wait_ge(b_ordered, 1)
                pe.transpose(b_ps[:, 2 * FC:4 * FC], b_by_feature,
                             ident[0:2 * FC, 0:2 * FC]).then_inc(b_turned, 1)

            def job(b, j, part):
                graph = (b, 1)
                if not exists(graph):
                    return
                bank = job_ps[BANK[j]]
                if part == 0 and (n := due(graph, JOBS, last_in_bank(j) + 1)) is not None:
                    pe.wait_ge(job_done, n)
                if j == ADJ_T:
                    pe.wait_ge(adj_loaded, due(graph, 16, 16))
                if starting(b):
                    for layer, first in enumerate((H1, S2, S3)):
                        if j == first:
                            pe.wait_ge(gcn_ready, layer + 1)
                    for n, first in enumerate((K0, Q0, V)):
                        if j == first:
                            pe.wait_ge(w_ready, FC * (n + 1))
                by_chunk = {AX: (0, 1, 2, 3), H1: (AX, AX + 1), S2: (H1, H1 + 1), H2: (S2, S2, S2 + 1, S2 + 1),
                            S3: (H2, H2 + 1), OUT3: (S3, S3, S3 + 1, S3 + 1), K0: (X_T, X_T + 1)}.get(j)
                sources = None if by_chunk is None else (graph, by_chunk)
                if j < AX:
                    for t in range(NT):
                        last = pe.transpose(bank[:, t * P:(t + 1) * P],
                                            adj_in[:, t, j * P:(j + 1) * P], ident[:])
                elif j < H1:
                    if j == AX and part == 0:
                        pe.wait_ge(x_hi, due(graph, 2, 2))
                        pe.wait_ge(x_lo, due(graph, NT, NT))
                    f = j - AX
                    last = three(bank[:], lambda i, m: xs[i][:, m, f * P:(f + 1) * P],
                                 lambda i, m: adjT[i][:, m, :], NT, part, PARTS[j], sources)
                elif j < S2:
                    f = j - H1
                    last = three(bank[:], lambda i, c: w_gcn[i][:, 0, c, f * P:(f + 1) * P],
                                 lambda i, c: axT_part[i][:, c, :], FC, sources=sources)
                elif j < H2 or S3 <= j < OUT3:
                    layer = 1 if j < H2 else 2
                    for t in range(2):
                        n = 2 * (j - (S2 if j < H2 else S3)) + t
                        last = three(bank[:, t * F:(t + 1) * F],
                                     lambda i, c: hids[i][:, c, n * P:(n + 1) * P],
                                     lambda i, c: w_gcn[i][:, layer, c, :], FC, sources=sources)
                elif j < S3:
                    f = j - H2
                    last = three(bank[:], lambda i, m: sup_part[i][:, m, f * P:(f + 1) * P],
                                 lambda i, m: adjT[i][:, m, :], NT, part, PARTS[j], sources)
                elif j < X_T:
                    n = j - OUT3
                    last = three(bank[:, 0:F],
                                 lambda i, m: adjT[i][:, m, n * P:(n + 1) * P],
                                 lambda i, m: sup_part[i][:, m, :], NT, sources=sources)
                elif j < K0:
                    for t in range(NT):
                        if j == X_T:
                            pe.wait_ge(xn_ready, due(graph, NT, t + 1))
                        last = pe.transpose(bank[:, t * P:(t + 1) * P],
                                            xn[:, t, (j - X_T) * P:(j - X_T + 1) * P], ident[:])
                elif j in (V, V + 1):
                    for t in range(2):
                        n = 2 * (j - V) + t
                        last = three(bank[:, t * F:(t + 1) * F],
                                     lambda i, c: hids[i][:, c, n * P:(n + 1) * P],
                                     lambda i, c: w_qkv[i][:, 2, c, :], FC)
                else:
                    g = 0 if j < V else 1
                    w = 0 if j in (Q0, Q1) else 1
                    last = three(bank[:], lambda i, c: w_qkv[i][:, w, c, g * P:(g + 1) * P],
                                 lambda i, c: hids[i][:, c, :], FC, sources=sources)
                if part == PARTS[j] - 1:
                    last.then_inc(job_made, 1)

            def scores(b, i):
                graph = (b, 0)
                if not exists(graph):
                    return
                step, h = divmod(i, GROUP)
                g, t = divmod(step, NT)
                if i % (SLOTS // GROUPS) == 0:
                    pe.wait_ge(stack_ready[g], due(graph, 16 * STACK_DMAS, 16 * STACK_DMAS))
                if (n := due(graph, SLOTS, i - 1)) is not None:
                    pe.wait_ge(masked_ready, n)
                head = GROUP * g + h
                pe.matmul(score_ps[i % 2][:], stack["q"][:, head, t * P:(t + 1) * P],
                          stack["k"][:, head, :], start=True, stop=True).then_inc(scores_made, 1)

            def turn(b, i):
                graph, k = ago(b, i, TRANSPOSE_LAG)
                if not exists(graph):
                    return
                pe.wait_ge(probs_ready, due(graph, SLOTS, k + 1))
                if (k - 2) % GROUP != VECTOR_HEAD:
                    if (n := due(graph, ACT_COPIES * STEPS, act_copies(k - 1))) is not None:
                        pe.wait_ge(copied_act, n)
                else:
                    if (n := due(graph, STEPS, vector_copies(k - 1))) is not None:
                        pe.wait_ge(copied_dve, n)
                for c in range(NT):
                    last = pe.transpose(turn_ps[k % 2][:, c * P:(c + 1) * P],
                                        probs[:, k % 4, c * P:(c + 1) * P], ident[:])
                last.then_inc(turned, 1)

            def context(b, i):
                if (i - PV_LAG) % GROUP:
                    return
                graph, k = ago(b, i, PV_LAG)
                if not exists(graph):
                    return
                step = k // GROUP
                g, t = divmod(step, NT)
                pe.wait_ge(copied_act, due(graph, ACT_COPIES * STEPS, ACT_COPIES * (step + 1)))
                pe.wait_ge(copied_dve, due(graph, STEPS, step + 1))
                if t == 0:
                    pe.wait_ge(v_ready[g], due(graph, 16, 16))
                if (n := due(graph, STEPS, step)) is not None:
                    pe.wait_ge(ctx_ready, n)
                if (n := due(graph, NT, max(step - NT, 0))) is not None:
                    pe.wait_ge(y2_ready, n)
                for c in range(NT):
                    for h in range(GROUP):
                        col = g * P + DH * h
                        pe.matmul(ctx_acc[DH * h:DH * (h + 1), :], v_use[:, c, col:col + DH],
                                  probsT[:, step % 2, h, c * P:(c + 1) * P],
                                  start=(c == 0), stop=(c == NT - 1), tile_position=(0, DH * h))
                pe.wait_ge(rinv_ready, due(graph, STEPS, step + 1))
                pe.transpose(rinv_ps, rinv_wide[:], ident[:]).then_inc(pv_made, 1)

            def out_product(b, i):
                if (i - WO_LAG) % GROUP:
                    return
                graph, k = ago(b, i, WO_LAG)
                step = k // GROUP
                g, t = divmod(step, NT)
                if not exists(graph) or g != GROUPS - 1:
                    return
                pe.wait_ge(ctx_ready, due(graph, STEPS, step + 1))
                if isinstance(b, int) and b == 0:
                    pe.wait_ge(w_ready, 3 * FC + 1)
                for e in range(FC):
                    last = pe.matmul(wo_ps, ctxT[:, e, t, :], w_o[:, e, :], start=(e == 0), stop=(e == FC - 1))
                last.then_inc(wo_made, 1)

            def iteration(b):
                for i in slots(b):
                    if starting(b):
                        for n, (w, turn_slot, _) in enumerate(QKVO):
                            if i == turn_slot:
                                turn_weights(n, w)
                    scores(b, i)
                    turn(b, i)
                    context(b, i)
                    out_first = K0 in jobs_in(i)
                    if out_first:
                        out_product(b, i)
                    for j, part in PLAN.get(i, []):
                        job(b, j, part)
                    if not out_first:
                        out_product(b, i)
                    if starting(b) and i == BIAS_SLOT:
                        turn_biases()

            pe.wait_ge(ident_ready, 1)
            iterations(pe, iteration, B - 2)

        @block.scalar
        def _(act):
            def copy_turned(b, i):
                graph, k = ago(b, i, TRANSPOSE_LAG)
                step, h = divmod(k, GROUP)
                if not exists(graph) or h == VECTOR_HEAD:
                    return
                act.wait_ge(turned, due(graph, SLOTS, k + 1))
                if (n := due(graph, STEPS, step - 1)) is not None:
                    act.wait_ge(pv_made, n)
                act.activation(probsT[:, step % 2, h, :], turn_ps[k % 2][:], ACT.Copy).then_inc(copied_act, 1)

            def exponentials(b, i):
                graph, k = ago(b, i, EXP_LAG)
                if not exists(graph):
                    return
                step, h = divmod(k, GROUP)
                act.wait_ge(shift_ready, due(graph, SLOTS, k + 1))
                if (n := due(graph, SLOTS, k - 3)) is not None:
                    act.wait_ge(turned, n)
                if h == 0 and (n := due(graph, STEPS, step - 1)) is not None:
                    act.wait_ge(rinv_raw, n)
                act.activation(probs[:, k % 4, :], masked[:, k % MASKED, :], ACT.Exp, bias=shift[:, h:h + 1],
                               scale=SCORE_SCALE, accum_out=rowsum[:, step % 2, h:h + 1]).then_inc(probs_ready, 1)

            def job(b, j):
                graph = (b, 1)
                if not exists(graph) or j in VECTOR_ONLY:
                    return
                bank = job_ps[BANK[j]][:]
                act.wait_ge(job_made, due(graph, JOBS, j + 1))
                if starting(b) and j == H1:
                    act.wait_ge(b_ready, 1)
                if j in RELU_JOBS:
                    layer, f = (0, j - H1) if j < S2 else (1, j - H2)
                    if (n := due(graph, JOBS, S2 if layer else H2 + 2 - JOBS)) is not None:
                        act.wait_ge(job_done, n)
                    act.activation(hid[:, f, :], bank, ACT.Relu, bias=b_cols[:, layer, f:f + 1]).then_inc(job_hi, 1)
                elif j in (K0, Q0, K1, Q1):
                    g = 0 if j < V else 1
                    t = "q" if j in (Q0, Q1) else "k"
                    if (n := due(graph, 16 * STACK_DMAS, 0)) is not None:
                        act.wait_ge(stack_ready[g], n)
                    act.activation(qk[t][0][:, g, :], bank, ACT.Identity,
                                   bias=b_cols[:, 2 + (t == "k"), g:g + 1]).then_inc(job_hi, 1)
                else:
                    act.activation(split_target(j)[0], bank, ACT.Copy).then_inc(job_hi, 1)

            def split_x(b, k):
                graph = (b, 2)
                if exists(graph):
                    act.wait_ge(x_loaded, due(graph, 16, 16))
                    if (n := due((b, 1), JOBS, AX + 2)) is not None:
                        act.wait_ge(job_made, n)
                    half = slice(2 * k, 2 * k + 2)
                    act.activation(xs[0][:, half, :], x_in[:, half, :], ACT.Copy).then_inc(x_hi, 1)

            def iteration(b):
                for i in slots(b):
                    copy_turned(b, i)
                    exponentials(b, i)
                    if i in SPLIT_X_SLOTS:
                        split_x(b, SPLIT_X_SLOTS.index(i))
                    for j in jobs_in(i):
                        job(b, j)
                    if starting(b) and i == GCN_SLOT:
                        act.wait_ge(gcn_loaded, 16 * 3)
                        for layer in range(3):
                            act.activation(w_gcn[0][:, layer, :, :], staged[:, layer, :, :],
                                           ACT.Copy).then_inc(gcn_hi, 1)

            for k in range(2):
                split_x(-2, k)
            iterations(act, iteration, B - 3)

        @block.vector
        def _(dve):
            def split_weights(n, w):
                turned_w = w_ps[n][:].rearrange("p (e f) -> p e f", e=FC)
                dve.wait_ge(w_turned, n + 1)
                if w == 3:
                    dve.tensor_copy(w_o[:], turned_w).then_inc(w_ready, 1)
                    return
                for e in range(FC):
                    order = "p (g h d) -> p g d h" if w < 2 else "p (g h d) -> p g h d"
                    hi, lo = (w_qkv[i][:, w, e, :].rearrange("p (g a b) -> p g a b", g=GROUPS,
                                                             a=DH if w < 2 else GROUP) for i in range(2))
                    src = turned_w[:, e, :].rearrange(order, g=GROUPS, h=GROUP)
                    dve.tensor_copy(hi, src).then_inc(w_hi, 1)
                    dve.wait_ge(w_hi, FC * n + e + 1)
                    dve.tensor_tensor(lo, src, hi.bitcast(F32), ALU.subtract).then_inc(w_ready, 1)

            def order_biases():
                dve.wait_ge(b_loaded, 16 * 7)
                dve.tensor_copy(b_by_feature.rearrange("n (d h) -> n d h", h=GROUP),
                                b_staged[:, 1, :].rearrange("n (h d) -> n d h", h=GROUP)).then_inc(b_ordered, 1)

            def keep_biases():
                dve.wait_ge(b_turned, 1)
                dve.tensor_copy(b_cols[:].rearrange("p n c -> p (n c)"), b_ps[:, 0:4 * FC]).then_inc(b_ready, 1)

            def mask_scores(b, i):
                graph = (b, 0)
                if not exists(graph):
                    return
                t = i // GROUP % NT
                made = held(dve, due(graph, SLOTS, i + 1))
                used = held(dve, due(graph, SLOTS, i + 1 - MASKED))
                loaded = held(dve, due(graph, 16, 16))
                dve.wait_ge(ident_ready, 1)
                dve.wait_ge(scores_made, made)
                if used is not None:
                    dve.wait_ge(probs_ready, used)
                if i % GROUP == 0 and i < SLOTS // GROUPS:
                    dve.wait_ge(mask_loaded[t], loaded)
                dve.tensor_tensor_reduce(masked[:, i % MASKED, :], score_ps[i % 2][:], mask[:, t, :], 1.0,
                                         float(np.finfo(np.float32).min), ALU.mult, ALU.max,
                                         rowmax[:, i % GROUP:i % GROUP + 1]).then_inc(masked_ready, 1)

            def copy_turned(b, i):
                graph, k = ago(b, i, TRANSPOSE_LAG)
                step, h = divmod(k, GROUP)
                if not exists(graph) or h != VECTOR_HEAD:
                    return
                dve.wait_ge(turned, due(graph, SLOTS, k + 1))
                if (n := due(graph, STEPS, step - 1)) is not None:
                    dve.wait_ge(pv_made, n)
                dve.tensor_copy(probsT[:, step % 2, h, :], turn_ps[k % 2][:]).then_inc(copied_dve, 1)

            def reciprocals(b, i):
                if (i - RINV_LAG) % GROUP:
                    return
                graph, k = ago(b, i, RINV_LAG)
                if not exists(graph):
                    return
                step = k // GROUP
                dve.wait_ge(probs_ready, due(graph, SLOTS, GROUP * (step + 1)))
                dve.reciprocal(rinv[:, step % 2, :], rowsum[:, step % 2, :]).then_inc(rinv_raw, 1)

            def widen_reciprocals(b, i):
                if (i - RINV_LAG) % GROUP:
                    return
                graph, k = ago(b, i, RINV_LAG)
                if not exists(graph):
                    return
                step = k // GROUP
                dve.wait_ge(rinv_raw, due(graph, STEPS, step + 1))
                if (n := due(graph, STEPS, step)) is not None:
                    dve.wait_ge(pv_made, n)
                dve.tensor_copy(rinv_wide[:].rearrange("p (h d) -> p h d", h=GROUP),
                                rinv[:, step % 2, :].unsqueeze(2).to_broadcast([P, GROUP, DH]))\
                    .then_inc(rinv_ready, 1)

            def copy_reciprocals(b, i):
                if (i - CTX_LAG) % GROUP:
                    return
                graph, k = ago(b, i, CTX_LAG)
                if not exists(graph):
                    return
                step = k // GROUP
                g, t = divmod(step, NT)
                dve.wait_ge(pv_made, due(graph, STEPS, step + 1))
                dve.tensor_copy(rinvT[:], rinv_ps).then_inc(rinvT_ready, 1)

            def normalise_context(b, i):
                if (i - CTX_LAG) % GROUP:
                    return
                graph, k = ago(b, i, CTX_LAG)
                if not exists(graph):
                    return
                step = k // GROUP
                g, t = divmod(step, NT)
                dve.wait_ge(rinvT_ready, due(graph, STEPS, step + 1))
                dve.tensor_tensor(ctxT[:, g, t, :], ctx_acc, rinvT[:], ALU.mult).then_inc(ctx_ready, 1)

            def residual2(b, i):
                if (i - Y2_LAG) % GROUP:
                    return
                graph, k = ago(b, i, Y2_LAG)
                g, t = divmod(k // GROUP, NT)
                if not exists(graph) or g != GROUPS - 1:
                    return
                dve.wait_ge(wo_made, due(graph, NT, t + 1))
                dve.wait_ge(res_ready, due(graph, NT, NT))
                dve.tensor_tensor(y2[:, t % 2, :], wo_ps, res[:, t, :], ALU.add).then_inc(y2_ready, 1)

            def moments2(b, i):
                if (i - STATS2_LAG) % GROUP:
                    return
                graph, k = ago(b, i, STATS2_LAG)
                g, t = divmod(k // GROUP, NT)
                if not exists(graph) or g != GROUPS - 1:
                    return
                dve.wait_ge(y2_ready, due(graph, NT, t + 1))
                dve.bn_stats(stats2[:, t % 2, :], y2[:, t % 2, :]).then_inc(stats2_ready, 1)

            def variance2(b, i):
                if (i - STATS2_LAG) % GROUP:
                    return
                graph, k = ago(b, i, STATS2_LAG)
                g, t = divmod(k // GROUP, NT)
                if not exists(graph) or g != GROUPS - 1:
                    return
                n = held(dve, due(graph, NT, t + 1))
                dve.wait_ge(ident_ready, 1)
                dve.wait_ge(stats2_ready, n)
                dve.bn_aggr(mv2[:, t % 2, :], stats2[:, t % 2, :]).then_inc(mv2_ready, 1)

            def normalise2(b, i):
                if (i - NORM2_LAG) % GROUP:
                    return
                graph, k = ago(b, i, NORM2_LAG)
                g, t = divmod(k // GROUP, NT)
                if not exists(graph) or g != GROUPS - 1:
                    return
                dve.wait_ge(rstd2_ready, due(graph, NT, t + 1))
                if (n := due(graph, 16 * NT // 2, 16 * (t // 2))) is not None:
                    dve.wait_ge(out_stored[t % 2], n)
                dve.tensor_scalar(out_sb[:, t % 2, :], y2[:, t % 2, :], mv2[:, t % 2, 0:1], rstd2[:, t % 2, 0:1],
                                  ALU.subtract, ALU.mult).then_inc(out_ready, 1)

            def job(b, j):
                graph = (b, 1)
                if not exists(graph):
                    return
                bank = job_ps[BANK[j]][:]
                if j in VECTOR_ONLY:
                    dve.wait_ge(job_made, due(graph, JOBS, j + 1))
                else:
                    dve.wait_ge(job_hi, due(graph, len(SCALAR_JOBS), scalar_count(j)))
                if j in RELU_JOBS:
                    f = j - (H1 if j < S2 else H2)
                    order = (H1, H1 + 1, H2, H2 + 1).index(j)
                    dve.tensor_copy(hids[0][:, f, :], hid[:, f, :]).then_inc(hid_hi, 1)
                    dve.wait_ge(hid_hi, due(graph, len(RELU_JOBS), order + 1))
                    dve.tensor_tensor(hids[1][:, f, :], hid[:, f, :], hids[0][:, f, :].bitcast(F32),
                                      ALU.subtract).then_inc(job_done, 1)
                elif j in (K0, Q0, K1, Q1):
                    g = 0 if j < V else 1
                    t = "q" if j in (Q0, Q1) else "k"
                    dve.scalar_tensor_tensor(out=qk[t][1][:, g, :], in0=bank,
                                             scalar=b_cols[:, 2 + (t == "k"), g:g + 1],
                                             in1=qk[t][0][:, g, :].bitcast(F32),
                                             op0=ALU.add, op1=ALU.subtract).then_inc(job_done, 1)
                elif j in (V, V + 1):
                    for g in range(GROUPS):
                        if (n := due(graph, 16, 0)) is not None:
                            dve.wait_ge(v_ready[g], n)
                    n = 2 * (j - V)
                    dve.tensor_tensor(v_new[:, n:n + 2, :], bank.rearrange("p (t f) -> p t f", t=2),
                                      b_rows[:, 1:2, :].to_broadcast([P, 2, F]), ALU.add).then_inc(job_done, 1)
                else:
                    hi, lo = split_target(j)
                    dve.tensor_tensor(lo, bank, hi.bitcast(F32), ALU.subtract).then_inc(job_done, 1)

            def residual1(b, t):
                graph = (b, 1)
                if not exists(graph):
                    return
                a, k = divmod(t, 2)
                dve.wait_ge(job_made, due(graph, JOBS, OUT3 + t + 1))
                dve.wait_ge(xb_ready, due(graph, NT, t + 1))
                dve.tensor_tensor(y1[:, a, k, :], job_ps[BANK[OUT3 + t]][:, 0:F], xb[:, t, :],
                                  ALU.add).then_inc(job_done, 1)

            def moments1(b, t):
                graph = (b, 1)
                if not exists(graph):
                    return
                a, k = divmod(t, 2)
                dve.wait_ge(job_done, due(graph, JOBS, OUT3 + t + 1))
                dve.bn_stats(stats1[:, a, k, :], y1[:, a, k, :]).then_inc(stats1_ready, 1)

            def variance1(b, t):
                graph = (b, 1)
                if not exists(graph):
                    return
                a, k = divmod(t, 2)
                n = held(dve, due(graph, NT, t + 1))
                dve.wait_ge(ident_ready, 1)
                dve.wait_ge(stats1_ready, n)
                dve.bn_aggr(mv1[:, a, k, :], stats1[:, a, k, :]).then_inc(mv1_ready, 1)

            def normalise1(b, a):
                graph = (b, 1)
                if not exists(graph):
                    return
                dve.wait_ge(rstd1_ready, due(graph, 2, a + 1))
                if (n := due(graph, NT, 0)) is not None:
                    dve.wait_ge(res_ready, n)
                for t in range(2):
                    dve.tensor_scalar(xn[:, 2 * a + t, :], y1[:, a, t, :], mv1[:, a, t, 0:1],
                                      rstd1[:, a, t:t + 1], ALU.subtract, ALU.mult).then_inc(xn_ready, 1)

            def iteration(b):
                for i in slots(b):
                    outs = [j - OUT3 for j in jobs_in(i) if OUT3 <= j < X_T]
                    if OUT3 + 3 in jobs_in(i - NORM1_LAG):
                        normalise1(b, 0)
                    mask_scores(b, i)
                    if OUT3 + 3 in jobs_in(i - NORM1_LAG):
                        normalise1(b, 1)
                    reciprocals(b, i)
                    copy_reciprocals(b, i)
                    copy_turned(b, i)
                    for t in outs:
                        residual1(b, t)
                    widen_reciprocals(b, i)
                    normalise_context(b, i)
                    for t in outs:
                        moments1(b, t)
                    residual2(b, i)
                    for j in jobs_in(i):
                        if not OUT3 <= j < X_T:
                            job(b, j)
                    moments2(b, i)
                    for t in outs:
                        variance1(b, t)
                    normalise2(b, i)
                    variance2(b, i)
                    if starting(b):
                        for n, (w, _, split_slot) in enumerate(QKVO):
                            if i == split_slot:
                                split_weights(n, w)
                        if i == BIAS_SLOT - 1:
                            order_biases()
                        if i == BIAS_SLOT:
                            keep_biases()

            iterations(dve, iteration, B - 2)

        @block.gpsimd
        def _(pool):
            pool.memset(ident[:], 0.0).then_inc(ident_zero, 1)
            pool.memset(minus_half[:], -0.5).then_inc(ident_zero, 1)
            pool.wait_ge(ident_zero, 2)
            pool.affine_select(out=ident[:], in_=ident[:], compare_op=ALU.not_equal, fill=1.0, base=0,
                               pattern=[[-1, P]], channel_multiplier=1).then_inc(ident_ready, 1)

            def shifts(b, i):
                graph = (b, 0)
                if exists(graph):
                    h = i % GROUP
                    n = held(pool, due(graph, SLOTS, i + 1))
                    pool.wait_ge(ident_ready, 1)
                    pool.wait_ge(masked_ready, n)
                    pool.tensor_scalar(shift[:, h:h + 1], rowmax[:, h:h + 1], -SCORE_SCALE, None,
                                       ALU.mult).then_inc(shift_ready, 1)

            def lo_of_x(b, t):
                graph = (b, 2)
                if exists(graph):
                    pool.wait_ge(x_hi, due(graph, 2, t // 2 + 1))
                    pool.tensor_tensor(xs[1][:, t, :], x_in[:, t, :], xs[0][:, t, :].bitcast(F32),
                                       ALU.subtract).then_inc(x_lo, 1)

            def x_with_bias(b, t):
                graph = (b, 2)
                if exists(graph):
                    if (n := due((b, 1), JOBS, X_T)) is not None:
                        pool.wait_ge(job_done, n)
                    pool.tensor_tensor(xb[:, t, :], x_in[:, t, :], b_rows[:, 0, :], ALU.add).then_inc(xb_ready, 1)

            def residual(b, t):
                graph = (b, 0)
                if exists(graph):
                    pool.wait_ge(xn_ready, due(graph, NT, NT))
                    if (n := due(graph, NT, 0)) is not None:
                        pool.wait_ge(y2_ready, n)
                    pool.tensor_tensor(res[:, t, :], xn[:, t, :], b_rows[:, 2, :], ALU.add).then_inc(res_ready, 1)

            def rstd_1(b, a):
                graph = (b, 1)
                if exists(graph):
                    n = held(pool, due(graph, NT, 2 * a + 2))
                    pool.wait_ge(ident_ready, 1)
                    pool.wait_ge(mv1_ready, n)
                    pool.tensor_scalar(ve1[:, a, :], mv1[:, a, :, 1], EPS, None, ALU.add).then_inc(ve1_ready, 1)
                    pool.wait_ge(ve1_ready, due(graph, 2, a + 1))
                    pool.tensor_tensor(rstd1[:, a, :], ve1[:, a, :], minus_half[:], ALU.pow).then_inc(rstd1_ready, 1)

            def rstd_2(b, i):
                if (i - STATS2_LAG) % GROUP:
                    return
                graph, k = ago(b, i, STATS2_LAG)
                g, t = divmod(k // GROUP, NT)
                if not exists(graph) or g != GROUPS - 1:
                    return
                n = held(pool, due(graph, NT, t + 1))
                pool.wait_ge(ident_ready, 1)
                pool.wait_ge(mv2_ready, n)
                pool.tensor_scalar(ve2[:, t % 2, :], mv2[:, t % 2, 1:2], EPS, None, ALU.add).then_inc(ve2_ready, 1)
                pool.wait_ge(ve2_ready, due(graph, NT, t + 1))
                pool.tensor_tensor(rstd2[:, t % 2, :], ve2[:, t % 2, :], minus_half[:, 0:1],
                                   ALU.pow).then_inc(rstd2_ready, 1)

            def iteration(b):
                for i in slots(b):
                    shifts(b, i)
                    rstd_2(b, i)
                    if i in LO_OF_X_SLOTS:
                        lo_of_x(b, LO_OF_X_SLOTS.index(i))
                    if i in X_WITH_BIAS_SLOTS:
                        x_with_bias(b, X_WITH_BIAS_SLOTS.index(i))
                    if i in RESIDUAL_SLOTS:
                        residual(b, RESIDUAL_SLOTS.index(i))
                    for a in range(2):
                        if OUT3 + 2 * a + 1 in jobs_in(i):
                            rstd_1(b, a)

            for t in range(NT):
                lo_of_x(-2, t)
            for layer in range(3):
                pool.wait_ge(gcn_hi, layer + 1)
                pool.tensor_tensor(w_gcn[1][:, layer, :, :], staged[:, layer, :, :],
                                   w_gcn[0][:, layer, :, :].bitcast(F32), ALU.subtract).then_inc(gcn_ready, 1)
            pool.wait_ge(b_loaded, 16 * 7)
            for t in range(NT):
                x_with_bias(-2, t)
            iterations(pool, iteration, B - 3)


_INS = ["x", "adj", "L0_gnn_W1", "L0_gnn_b1", "L0_gnn_W2", "L0_gnn_b2", "L0_gnn_W3", "L0_gnn_b3",
        "L1_gnn_Wq", "L1_gnn_bq", "L1_gnn_Wk", "L1_gnn_bk", "L1_gnn_Wv", "L1_gnn_bv", "L1_gnn_Wo", "L1_gnn_bo"]


def kernel(**inputs):
    import concourse.bacc as _bacc
    from concourse.bass_utils import run_bass_kernel_spmd as _run

    nc = _bacc.Bacc("TRN2", target_bir_lowering=False, num_devices=1)
    arrays, args = {}, []
    for name in _INS:
        a = np.ascontiguousarray(inputs[name])
        arrays[f"in_{name}"] = a
        args.append(nc.dram_tensor(f"in_{name}", a.shape, mybir.dt.from_np(a.dtype), kind="ExternalInput").ap())
    out = nc.dram_tensor("out", inputs["x"].shape, F32, kind="ExternalOutput").ap()
    gcn_attention_kernel(nc, *args, out)
    r = _run(nc, [arrays], core_ids=[0])
    return r.results[0]["out"]
```
